# Optimizing a Trainium2 kernel written in Bass

```python
import numpy as np
import jax
import jax.numpy as jnp

def _softmax(x, axis=-1):
    return jax.nn.softmax(x, axis=axis)

def _gelu(x):
    return jax.nn.gelu(x, approximate=True)

def _silu(x):
    return jax.nn.silu(x)

def _sigmoid(x):
    return jax.nn.sigmoid(x)

def _layernorm(x, axis=-1, eps=1e-05):
    m = jnp.mean(x, axis=axis, keepdims=True)
    v = jnp.var(x, axis=axis, keepdims=True)
    return (x - m) / jnp.sqrt(v + eps)

def _scatter_add(tgt, idx, src, axis=0):
    return tgt.at[idx].add(src)

def _segment_sum(src, seg, n):
    return jax.ops.segment_sum(src, seg, n)
kernel_name = 'mk_conv_seq_d1_conv_nhwc192_r4_ff4c45'

def setup_inputs(seed: int=0):
    np.random.seed(seed)
    _w = jnp.asarray

    def _rec_inputs():
        import jax
        import jax.numpy as jnp
        _gk = jax.random.key(seed)
        x = -0.0001476 + 0.9999 * jax.random.normal(jax.random.fold_in(_gk, 1), (16, 56, 56, 48), jnp.float32)
        return x
    x = _rec_inputs()

    def _L0_conv_setup():
        import jax, jax.numpy as jnp
        import numpy as np
        B = 16
        H = 56
        W = 56
        C = 48
        WS = 7
        SS = 3
        NH = 6
        N = WS * WS
        HD = C // NH
        HID = 4 * C
        NW = H // WS * (W // WS)
        SCALE = HD ** (-0.5)
        EPS = 1e-05

        def _rel_pos_index():
            coords = np.stack(np.meshgrid(np.arange(WS), np.arange(WS), indexing='ij'))
            cf = coords.reshape(2, -1)
            rel = (cf[:, :, None] - cf[:, None, :]).transpose(1, 2, 0)
            rel[:, :, 0] += WS - 1
            rel[:, :, 1] += WS - 1
            rel[:, :, 0] *= 2 * WS - 1
            return jnp.asarray(rel.sum(-1))

        def _attn_mask():
            img = np.zeros((H, W))
            cnt = 0
            for hs in (slice(0, -WS), slice(-WS, -SS), slice(-SS, None)):
                for ws in (slice(0, -WS), slice(-WS, -SS), slice(-SS, None)):
                    img[hs, ws] = cnt
                    cnt += 1
            mw = img.reshape(H // WS, WS, W // WS, WS).transpose(0, 2, 1, 3).reshape(-1, N)
            am = mw[:, None, :] - mw[:, :, None]
            return jnp.asarray(np.where(am != 0, -100.0, 0.0).astype(np.float32))
        RPI = _rel_pos_index()
        MASK = _attn_mask()

        def _ln(x, g, b):
            m = jnp.mean(x, -1, keepdims=True)
            v = jnp.mean(jnp.square(x - m), -1, keepdims=True)
            return (x - m) / jnp.sqrt(v + EPS) * g + b
        key = jax.random.key(seed)
        ks = jax.random.split(key, 16)
        f = jax.random.normal
        return {'x': f(ks[0], (B, H, W, C), jnp.float32), 'norm1_g': jnp.ones((C,), jnp.float32), 'norm1_b': jnp.zeros((C,), jnp.float32), 'qkv_w': f(ks[1], (C, 3 * C), jnp.float32) * 0.02, 'qkv_b': jnp.zeros((3 * C,), jnp.float32), 'rpb_table': f(ks[2], ((2 * WS - 1) * (2 * WS - 1), NH), jnp.float32) * 0.02, 'proj_w': f(ks[3], (C, C), jnp.float32) * 0.02, 'proj_b': jnp.zeros((C,), jnp.float32), 'norm2_g': jnp.ones((C,), jnp.float32), 'norm2_b': jnp.zeros((C,), jnp.float32), 'fc1_w': f(ks[4], (C, HID), jnp.float32) * 0.02, 'fc1_b': jnp.zeros((HID,), jnp.float32), 'fc2_w': f(ks[5], (HID, C), jnp.float32) * 0.02, 'fc2_b': jnp.zeros((C,), jnp.float32)}
    _L0_conv_all = _L0_conv_setup()
    _L0_conv_in = {k: v for k, v in _L0_conv_all.items() if k in ('norm1_g', 'norm1_b', 'qkv_w', 'qkv_b', 'rpb_table', 'proj_w', 'proj_b', 'norm2_g', 'norm2_b', 'fc1_w', 'fc1_b', 'fc2_w', 'fc2_b')}
    del _L0_conv_all
    return {'x': x, 'L0_conv_norm1_g': _L0_conv_in['norm1_g'], 'L0_conv_norm1_b': _L0_conv_in['norm1_b'], 'L0_conv_qkv_w': _L0_conv_in['qkv_w'], 'L0_conv_qkv_b': _L0_conv_in['qkv_b'], 'L0_conv_rpb_table': _L0_conv_in['rpb_table'], 'L0_conv_proj_w': _L0_conv_in['proj_w'], 'L0_conv_proj_b': _L0_conv_in['proj_b'], 'L0_conv_norm2_g': _L0_conv_in['norm2_g'], 'L0_conv_norm2_b': _L0_conv_in['norm2_b'], 'L0_conv_fc1_w': _L0_conv_in['fc1_w'], 'L0_conv_fc1_b': _L0_conv_in['fc1_b'], 'L0_conv_fc2_w': _L0_conv_in['fc2_w'], 'L0_conv_fc2_b': _L0_conv_in['fc2_b']}

def reference(x, L0_conv_norm1_g, L0_conv_norm1_b, L0_conv_qkv_w, L0_conv_qkv_b, L0_conv_rpb_table, L0_conv_proj_w, L0_conv_proj_b, L0_conv_norm2_g, L0_conv_norm2_b, L0_conv_fc1_w, L0_conv_fc1_b, L0_conv_fc2_w, L0_conv_fc2_b):
    import jax
    import jax.numpy as jnp

    def _L0_conv_ref(x, norm1_g, norm1_b, qkv_w, qkv_b, rpb_table, proj_w, proj_b, norm2_g, norm2_b, fc1_w, fc1_b, fc2_w, fc2_b):
        import jax, jax.numpy as jnp
        import numpy as np
        B = 16
        H = 56
        W = 56
        C = 48
        WS = 7
        SS = 3
        NH = 6
        N = WS * WS
        HD = C // NH
        HID = 4 * C
        NW = H // WS * (W // WS)
        SCALE = HD ** (-0.5)
        EPS = 1e-05

        def _rel_pos_index():
            coords = np.stack(np.meshgrid(np.arange(WS), np.arange(WS), indexing='ij'))
            cf = coords.reshape(2, -1)
            rel = (cf[:, :, None] - cf[:, None, :]).transpose(1, 2, 0)
            rel[:, :, 0] += WS - 1
            rel[:, :, 1] += WS - 1
            rel[:, :, 0] *= 2 * WS - 1
            return jnp.asarray(rel.sum(-1))

        def _attn_mask():
            img = np.zeros((H, W))
            cnt = 0
            for hs in (slice(0, -WS), slice(-WS, -SS), slice(-SS, None)):
                for ws in (slice(0, -WS), slice(-WS, -SS), slice(-SS, None)):
                    img[hs, ws] = cnt
                    cnt += 1
            mw = img.reshape(H // WS, WS, W // WS, WS).transpose(0, 2, 1, 3).reshape(-1, N)
            am = mw[:, None, :] - mw[:, :, None]
            return jnp.asarray(np.where(am != 0, -100.0, 0.0).astype(np.float32))
        RPI = _rel_pos_index()
        MASK = _attn_mask()

        def _ln(x, g, b):
            m = jnp.mean(x, -1, keepdims=True)
            v = jnp.mean(jnp.square(x - m), -1, keepdims=True)
            return (x - m) / jnp.sqrt(v + EPS) * g + b
        shortcut = x
        xn = _ln(x, norm1_g, norm1_b)
        xs = jnp.roll(xn, (-SS, -SS), axis=(1, 2))
        xw = xs.reshape(B, H // WS, WS, W // WS, WS, C).transpose(0, 1, 3, 2, 4, 5).reshape(-1, N, C)
        qkv = (xw @ qkv_w + qkv_b).reshape(-1, N, 3, NH, HD).transpose(2, 0, 3, 1, 4)
        q, k, v = (qkv[0], qkv[1], qkv[2])
        attn = jnp.einsum('bhnd,bhmd->bhnm', q * SCALE, k)
        rpb = rpb_table[RPI.reshape(-1)].reshape(N, N, NH).transpose(2, 0, 1)
        attn = attn + rpb[None]
        attn = attn.reshape(B, NW, NH, N, N) + MASK[None, :, None]
        attn = jax.nn.softmax(attn.reshape(-1, NH, N, N), axis=-1)
        out = jnp.einsum('bhnm,bhmd->bnhd', attn, v).reshape(-1, N, C)
        out = out @ proj_w + proj_b
        out = out.reshape(B, H // WS, W // WS, WS, WS, C).transpose(0, 1, 3, 2, 4, 5).reshape(B, H, W, C)
        out = jnp.roll(out, (SS, SS), axis=(1, 2))
        x1 = shortcut + out
        h = _ln(x1, norm2_g, norm2_b)
        h = jax.nn.gelu(h @ fc1_w + fc1_b, approximate=False)
        h = h @ fc2_w + fc2_b
        return x1 + h

    def _gn(v, G=32, eps=1e-05):
        B_, H_, W_, C_ = v.shape
        g = v.reshape(B_, H_, W_, G, C_ // G)
        m = jnp.mean(g, axis=(1, 2, 4), keepdims=True)
        s = jnp.var(g, axis=(1, 2, 4), keepdims=True)
        return ((g - m) / jnp.sqrt(s + eps)).reshape(v.shape)

    def _ln_c(v, eps=1e-06):
        m = jnp.mean(v, axis=-1, keepdims=True)
        s = jnp.var(v, axis=-1, keepdims=True)
        return (v - m) / jnp.sqrt(s + eps)

    def _ln_t(v, eps=1e-05):
        m = jnp.mean(v, axis=-1, keepdims=True)
        s = jnp.var(v, axis=-1, keepdims=True)
        return (v - m) / jnp.sqrt(s + eps)

    def _to_tokens(v):
        B_, H_, W_, C_ = v.shape
        return v.reshape(B_, H_ * W_, C_)

    def _from_tokens(t, like):
        return t.reshape(like.shape)
    x = _L0_conv_ref(x, L0_conv_norm1_g, L0_conv_norm1_b, L0_conv_qkv_w, L0_conv_qkv_b, L0_conv_rpb_table, L0_conv_proj_w, L0_conv_proj_b, L0_conv_norm2_g, L0_conv_norm2_b, L0_conv_fc1_w, L0_conv_fc1_b, L0_conv_fc2_w, L0_conv_fc2_b)
    return x

_drawn_inputs = setup_inputs


def setup_inputs(seed=0):
    import zlib

    import numpy as np

    out = dict(_drawn_inputs(seed))
    spreads = {'L0_conv_norm1_g': (1.0, 0.6),
     'L0_conv_norm1_b': (0.0, 0.8),
     'L0_conv_qkv_b': (0.0, 0.707),
     'L0_conv_proj_b': (0.0, 0.1),
     'L0_conv_norm2_g': (1.0, 0.6),
     'L0_conv_norm2_b': (0.0, 0.8),
     'L0_conv_fc1_b': (0.0, 0.447),
     'L0_conv_fc2_b': (0.0, 0.1)}
    factors = {'L0_conv_qkv_w': 8.0,
     'L0_conv_rpb_table': 8.0,
     'L0_conv_proj_w': 4.682,
     'L0_conv_fc1_w': 2.778}
    for name, (base, spread) in spreads.items():
        noise = np.random.default_rng([zlib.crc32(name.encode()), seed]).standard_normal(out[name].shape)
        drawn = base * np.exp(spread * noise) if base else spread * noise
        out[name] = jnp.asarray(drawn.astype(out[name].dtype))
    for name, factor in factors.items():
        out[name] = (out[name] * factor).astype(out[name].dtype)
    return out
```

```python
import numpy as np
import concourse.bass as bass
from concourse import mybir
from contextlib import ExitStack

B, H, W, C = 16, 56, 56, 48
WS, SS, NH = 7, 3, 6
N = WS * WS
HD = C // NH
HID = 4 * C
NWX = W // WS
EPS = 1e-5

UW = 16
UNITS = B * (H // WS) * NWX // UW
EDGE = UNITS - UNITS // (H // WS)
TOK = UW * N
CH = 7
PT = TOK // CH
HALF = TOK // 2
PAIRS = UW // 2
G, HP = 2, 3
GP = 64
AP_ = GP + N
KD = HP * HD
KQ = 32
KR = 2 * KQ + KD
MROW = 96
HL = 2 * C + 1
COLS = HP * N
CP = 9

SX, SWT = 4096.0, 64.0
SQ = 16.0
SO = 256.0
SB = SQ * SQ
SM = 16384.0

WQ = [0, KR]
WK = [2 * KR, 3 * KR]
WV = 4 * KR
WF1 = WV + C
WP = WF1 + HID
WCOLS = WP + C


def swin_block_kernel(nc, x, weights, gains, shifts, w2, b2, rpb, consts, maskt, ident, onescol, out):
    f32, f16 = mybir.dt.float32, mybir.dt.float16
    ALU, ACT, AX = mybir.AluOpType, mybir.ActivationFunctionType, mybir.AxisListType
    ctx = ExitStack()
    with ctx:
        def sb(name, shape, dt):
            return ctx.enter_context(nc.sbuf_tensor(name, shape, dt))

        def sem(name):
            return ctx.enter_context(nc.semaphore(name))

        xres = sb("xres", [PT, UNITS, CH * C], f32)
        nmean = sb("nmean", [PT, CH], f32)
        xc = sb("xc", [PT, CH, C], f32)
        sq = sb("sq", [PT, CH, C], f32)
        ssum = sb("ssum", [PT, CH], f32)
        var = sb("var", [PT, CH], f32)
        rstd = sb("rstd", [PT, CH], f32)
        mhalf = sb("mhalf", [PT, CH], f32)
        xn = sb("xn", [PT, CH, C], f32)
        xtok = sb("xtok", [PT, CH, HL], f16)
        xT = sb("xT", [HL, TOK], f16)
        w32 = sb("w32", [HL, WCOLS], f32)
        wh = sb("wh", [HL, WCOLS], f16)
        wl = sb("wl", [HL, WCOLS], f16)
        gain = sb("gain", [2 * C, 2], f32)
        shift = sb("shift", [C, 2, HL], f32)
        w2a = sb("w2a", [128, C], f32)
        w2b = sb("w2b", [128, 2, C], f32)
        b2t = sb("b2t", [PT, C], f32)
        rpb32 = sb("rpb32", [AP_, 2, COLS], f32)
        mask32 = sb("mask32", [AP_, 4, COLS], f32)
        biasr = sb("biasr", [AP_, 4, COLS], f32)
        bs_h = sb("bs_h", [AP_, 4, COLS], f16)
        bt_h = sb("bt_h", [AP_, 4, COLS], f16)
        bt_l = sb("bt_l", [AP_, 4, COLS], f16)
        idt = sb("idt", [128, 128], f16)
        headrow = sb("headrow", [KR, HP], f32)
        Qd = [sb(f"Qd{i}", [MROW + 1, G, UW, N], f16) for i in range(2)]
        Kd = [sb(f"Kd{i}", [MROW + 1, G, UW, N], f16) for i in range(2)]
        Qb = [sb(f"Qb{i}", [MROW + 1, G, HP, UW, N], f16) for i in range(2)]
        Kb = [sb(f"Kb{i}", [MROW + 1, G, HP, UW, N], f16) for i in range(2)]
        Vb = [sb(f"Vb{i}", [AP_, UW * HP, G * CP], f32) for i in range(2)]
        rowmax = sb("rowmax", [AP_, UW, HP], f32)
        m16 = sb("m16", [AP_, MROW], f16)
        mT = sb("mT", [HP * UW, AP_], f16)
        probs = [sb(f"probs{i}", [AP_, 2 * COLS], f32) for i in range(4)]
        rsum = sb("rsum", [AP_, PAIRS * NH], f32)
        on = sb("on", [AP_, PAIRS, C], f32)
        otok = sb("otok", [AP_, PAIRS, HL], f16)
        OT = sb("OT", [HL, UW, N], f16)
        gel = [sb(f"gel{i}", [128, 3, 4 * PT], f32) for i in range(2)]
        ybuf = [sb(f"ybuf{i}", [PT, CH * C], f32) for i in range(2)]

        banks = [ctx.enter_context(nc.psum_tensor(f"bank{i}", [128, 512], f32)) for i in range(7)]
        psT = ctx.enter_context(nc.psum_tensor("psT", [128, 1024], f16))
        lin, sc, st, po = banks[0:2], banks[2:4], banks[4:6], banks[6]

        s_x = [sem(f"x_loaded{i}") for i in range(2)]
        s_const = sem("constants_loaded")
        s_prep = sem("weights_prepared")
        s_prep_p = sem("shift_products")
        s_mean = sem("mean_ready")
        s_xc = sem("centred")
        s_sq = sem("squared")
        s_var = sem("variance_ready")
        s_pow = sem("rstd_ready")
        s_xn = sem("normalized")
        s_xhi = sem("x_high_ready")
        s_xlo = sem("x_low_ready")
        s_xtp = sem("x_transposed")
        s_xT = sem("xT_ready")
        s_qk = [sem(f"lin{i}_full") for i in range(2)]
        s_qkh = sem("qk_high_ready")
        s_linfree = [sem(f"lin{i}_free") for i in range(2)]
        s_qk_ready = sem("qk_operands_ready")
        s_s = sem("scores_full")
        s_max = sem("rowmax_ready")
        s_m16 = sem("m16_ready")
        s_mtp = sem("m_transposed")
        s_mT = sem("mT_ready")
        s_mrow = sem("m_row_written")
        s_st = sem("tscores_full")
        s_exp = sem("probs_ready")
        s_pv = sem("pv_done")
        s_rsum = sem("rsum_ready")
        s_norm = sem("attention_normalized")
        s_ohi = sem("o_high_ready")
        s_olo = sem("o_low_ready")
        s_otp = sem("o_transposed")
        s_OT = sem("OT_ready")
        s_dve = sem("vector_chain")
        s_h = sem("hidden_full")
        s_g = sem("gelu_ready")
        s_x1b = sem("x1_with_bias")
        s_y = sem("y_full")
        s_yo = sem("y_ready")
        s_store = [sem(f"stored{i}") for i in range(2)]

        NCONST = 16 * 12

        def used(b, t):
            if isinstance(t, int) and t == 0:
                return 0
            return 6 * t - 1 if b == 0 else 5 * t

        block = ctx.enter_context(nc.Block())

        def attention_phase(e, part):
            def step(t, par, edge, edge_b, first=False, last=False):
                part(e, t, par, edge, edge_b, first, last)
            step(0, 0, False, False, first=True)
            step(1, 1, False, False)
            with e.Fori(2, EDGE - 1, 2) as i:
                step(i, 0, False, False)
                step(i + 1, 1, False, False)
            step(EDGE, 0, True, False)
            with e.Fori(EDGE + 1, UNITS - 2, 2) as i:
                step(i, 1, True, True)
                step(i + 1, 0, True, True)
            step(UNITS - 1, 1, True, True)
            step(UNITS, 0, True, True, last=True)

        def mlp_phase(e, unit):
            for u in range(4):
                unit(u, u % 2, u < 2)
            with e.Fori(4, UNITS - 1, 2) as i:
                unit(i, 0, False)
                unit(i + 1, 1, False)

        @block.sync
        def _(sp):
            sp.dma_start(w32[:, :], weights).then_inc(s_const, 16)
            sp.dma_start(gain[:, :], gains).then_inc(s_const, 16)
            sp.dma_start(shift[:, :, :], shifts).then_inc(s_const, 16)
            sp.dma_start(w2a[:, :], w2[:, 0, :]).then_inc(s_const, 16)
            sp.dma_start(w2b[:, :, :], w2[:, 1:3, :]).then_inc(s_const, 16)
            sp.dma_start(b2t[:, :], b2).then_inc(s_const, 16)
            sp.dma_start(rpb32[:, :, :], rpb).then_inc(s_const, 16)
            sp.dma_start(mask32[:, :, :], maskt).then_inc(s_const, 16)
            sp.dma_start(idt[:, :], ident).then_inc(s_const, 16)
            sp.dma_start(headrow[:, :], consts).then_inc(s_const, 16)
            for i in range(2):
                sp.dma_start(Vb[i][:, :, :], onescol).then_inc(s_const, 16)

            def load(u, par, second=True):
                if second:
                    sp.wait_ge(s_x[par], 8 * (u - par))
                sp.dma_start(xres[:, bass.ds(u, 1), :], x[bass.ds(u, 1), :, :].rearrange("u p n -> p u n")).then_inc(s_x[par], 16)
            load(0, 0, False)
            load(1, 1, False)
            load(2, 0)

            def step(sp, t, par, edge, edge_b, first, last):
                if last:
                    return
                if not edge:
                    load(t + 3, 1 - par)
                elif isinstance(t, int) and t == EDGE:
                    for u in range(EDGE + 3, UNITS):
                        load(u, u % 2)
                sp.wait_ge(s_mT, t + 1)
                for g in range(G):
                    sp.dma_start(Qb[par][MROW:MROW + 1, g, :, :, :].rearrange("o a w n -> o (a w) n"),
                                 mT[:, g * GP:g * GP + N]).then_inc(s_mrow, 16)
            attention_phase(sp, step)

            def unit(u, par, first):
                sp.wait_ge(s_yo, u + 1)
                sp.dma_start(out[bass.ds(u, 1), :, :].rearrange("u p n -> p (u n)"), ybuf[par][:, :]).then_inc(s_store[par], 16)
            mlp_phase(sp, unit)
            for par in range(2):
                sp.wait_ge(s_store[par], 16 * UNITS // 2)

        def x_of(u):
            return xres[:, bass.ds(u, 1), :].rearrange("p u (c n) -> p (u c) n", n=C)

        @block.gpsimd
        def _(pool):
            nc.gpsimd.memset(mhalf[:, :], -0.5).then_inc(s_pow, 1)
            pool.wait_ge(s_pow, 1)
            pool.wait_ge(s_const, NCONST)

            def centre(u, n):
                pool.wait_ge(s_mean, n)
                nc.gpsimd.tensor_tensor(xc[:, :, :], x_of(u), nmean[:, :].unsqueeze(2).to_broadcast([PT, CH, C]),
                                        ALU.add).then_inc(s_xc, 1)

            def scale(n):
                pool.wait_ge(s_var, n)
                nc.gpsimd.tensor_tensor(rstd[:, :], var[:, :], mhalf[:, :], ALU.pow).then_inc(s_pow, 1)
                pool.wait_ge(s_pow, n + 1)
                nc.gpsimd.tensor_tensor(xn[:, :, :], xc[:, :, :], rstd[:, :].unsqueeze(2).to_broadcast([PT, CH, C]),
                                        ALU.mult).then_inc(s_xn, 1)

            centre(0, 1)
            scale(1)
            with pool.Fori(1, UNITS) as i:
                centre(i, i + 1)
                scale(i + 1)

            with pool.Fori(0, UNITS) as i:
                centre(i, i + UNITS + 1)
                nc.gpsimd.tensor_tensor(x_of(i), x_of(i), b2t[:, :].unsqueeze(1).to_broadcast([PT, CH, C]),
                                        ALU.add).then_inc(s_x1b, 1)
                scale(i + UNITS + 1)

        @block.scalar
        def _(act):
            def square(n):
                act.wait_ge(s_xc, n)
                nc.scalar.activation(sq[:, :, :], xc[:, :, :], ACT.Square).then_inc(s_sq, 1)

            def x_high(n, tp):
                act.wait_ge(s_xn, n)
                if tp is not None:
                    act.wait_ge(s_xtp, tp)
                nc.scalar.activation(xtok[:, :, 0:C], xn[:, :, :], ACT.Copy, scale=SX).then_inc(s_xhi, 1)

            def xT_copy(n):
                act.wait_ge(s_xtp, n)
                nc.scalar.activation(xT[:, :], psT[0:HL, 0:TOK], ACT.Copy).then_inc(s_xT, 1)

            def step(act, t, par, edge, edge_b, first, last):
                if first:
                    act.wait_ge(s_prep, 1)
                    square(1)
                    x_high(1, None)
                front = not last
                back = not first
                if front:
                    xT_copy(t + 1)

                def qk_high(j):
                    ten, g, half = (Kd, Qd)[j // 2 % 2][par], j // 4, j % 2
                    b = j % 2
                    act.wait_ge(s_qk[b], used(b, t) + j // 2 + 1)
                    nc.scalar.activation(ten[0:KR, g, half * 8:half * 8 + 8, :].rearrange("p w n -> p (w n)"),
                                         lin[b][0:KR, 0:HALF], ACT.Copy, scale=SQ / (SX * SWT)).then_inc(s_qkh, 1)

                def v_copy(j):
                    b = j
                    act.wait_ge(s_qk[b], used(b, t) + 5)
                    src = lin[b][0:N, 0:8 * C].rearrange("p (a g d) -> p a g d", g=G, d=HD)
                    for g in range(G):
                        i = nc.scalar.activation(Vb[par][g * GP:g * GP + N, 8 * HP * j:8 * HP * (j + 1), g * CP:g * CP + HD],
                                                 src[:, :, g, :], ACT.Copy, scale=1.0 / (SX * SWT))
                    i.then_inc(s_linfree[j], 1)

                def exp(p):
                    act.wait_ge(s_st, PAIRS * (t - 1) + p + 1)
                    if not (isinstance(t, int) and t == 1 and p < 4):
                        act.wait_ge(s_pv, PAIRS * (t - 1) + p - 3)
                    nc.scalar.activation(probs[p % 4][:, :], st[p % 2][0:AP_, 0:2 * COLS], ACT.Exp,
                                         scale=1.0 / SB).then_inc(s_exp, 1)

                if front:
                    if not (isinstance(t, int) and t < 2):
                        act.wait_ge(s_pv, PAIRS * (t - 1))
                    qk_high(0)
                for p in range(PAIRS):
                    if back:
                        exp(p)
                    if front and p + 1 < 8:
                        qk_high(p + 1)
                    if front and p == 3 and has_next(t):
                        square(t + 2)
                if front:
                    v_copy(0)
                    v_copy(1)
                if back:
                    act.wait_ge(s_norm, t)
                    nc.scalar.activation(otok[:, :, 0:C], on[:, :, :], ACT.Copy, scale=SO).then_inc(s_ohi, 1)
                    act.wait_ge(s_otp, t)
                    nc.scalar.activation(OT[:, :, :], psT[0:HL, :].rearrange("p (w n) -> p w n", n=GP)[:, :, 0:N],
                                         ACT.Copy).then_inc(s_OT, 1)
                if front and has_next(t):
                    x_high(t + 2, t + 1)

            def has_next(t):
                return not (isinstance(t, int) and t >= UNITS - 1)

            attention_phase(act, step)

            def unit(u, par, first):
                n = u + UNITS + 1
                square(n)
                x_high(n, n - 1)
                xT_copy(n)
                for k in range(3):
                    act.wait_ge(s_h, 3 * u + k + 1)
                    if k == 0 and not first:
                        act.wait_ge(s_y, u - 1)
                    hb = banks[3 * par + k]
                    if k < 2:
                        cols = (4 if k == 0 else 3) * PT
                        i = nc.scalar.activation(gel[par][:, k, 0:cols], hb[:, 0:cols], ACT.Gelu, scale=1.0 / (SX * SWT))
                    else:
                        nc.scalar.activation(gel[par][:, k, 0:3 * PT], hb[:, 0:3 * PT], ACT.Gelu, scale=1.0 / (SX * SWT))
                        i = nc.scalar.activation(gel[par][0:64, k, 3 * PT:4 * PT], hb[0:64, 3 * PT:4 * PT], ACT.Gelu,
                                                 scale=1.0 / (SX * SWT))
                    i.then_inc(s_g, 1)
            mlp_phase(act, unit)

        @block.tensor
        def _(pe):
            pe.wait_ge(s_const, NCONST)
            nc.tensor.matmul(lin[0][0:HL, 0:WF1], shift[:, 0, :], w32[0:C, 0:WF1], start=True, stop=True).then_inc(s_prep_p, 1)
            nc.tensor.matmul(lin[1][0:HL, 0:HID], shift[:, 1, :], w32[0:C, WF1:WP], start=True, stop=True).then_inc(s_prep_p, 1)
            pe.wait_ge(s_prep, 1)

            def x_transposes(n):
                pe.wait_ge(s_xlo, n)
                for c in range(CH):
                    i = nc.tensor.transpose(psT[0:HL, c * PT:(c + 1) * PT], xtok[:, c, :], idt[0:PT, 0:PT])
                i.then_inc(s_xtp, 1)

            def split_mm(dst, l_hi, l_lo, rhs):
                nc.tensor.matmul(dst, l_hi, rhs, start=True, stop=False)
                return nc.tensor.matmul(dst, l_lo, rhs, start=False, stop=True)

            def step(pe, t, par, edge, edge_b, first, last):
                front, back = not last, not first
                obar = 1 - par

                def lin_free(b, k):
                    if not (isinstance(t, int) and t == 0 and k == 0):
                        pe.wait_ge(s_linfree[b], used(b, t) + k)

                if front:
                    if back:
                        pe.wait_ge(s_mT, t)
                    x_transposes(t + 1)

                def qk_piece(j):
                    col, half, b = (WK, WQ)[j // 2 % 2][j // 4], j % 2, j % 2
                    lin_free(b, j // 2)
                    split_mm(lin[b][0:KR, 0:HALF], wh[:, col:col + KR], wl[:, col:col + KR],
                             xT[:, half * HALF:(half + 1) * HALF]).then_inc(s_qk[b], 1)

                def v_piece(j):
                    lin_free(j, 4)
                    for w in range(8):
                        tok = xT[:, (8 * j + w) * N:(8 * j + w + 1) * N]
                        dst = lin[j][0:N, w * C:(w + 1) * C]
                        nc.tensor.matmul(dst, tok, wh[:, WV:WV + C], start=True, stop=False)
                        i = nc.tensor.matmul(dst, tok, wl[:, WV:WV + C], start=False, stop=True)
                    i.then_inc(s_qk[j], 1)

                def t_scores(p):
                    bank = st[p % 2]
                    if not (isinstance(t, int) and t == 1 and p < 2):
                        pe.wait_ge(s_exp, PAIRS * (t - 1) + p - 1)
                    ty = 2 * edge_b
                    bias_pair(bank, bt_h, ty, p, True)
                    bias_pair(bank, bt_l, ty, p, False)
                    for w in range(2):
                        for g in range(G):
                            i = nc.tensor.matmul(bank[g * GP:g * GP + N, w * COLS:(w + 1) * COLS],
                                                 Kd[obar][:, g, 2 * p + w, :], Qb[obar][:, g, :, 2 * p + w, :],
                                                 start=False, stop=True, skip_group_check=True)
                    i.then_inc(s_st, 1)

                def pv(p):
                    pe.wait_ge(s_exp, PAIRS * (t - 1) + p + 1)
                    if p == 0 and not (isinstance(t, int) and t == 1):
                        pe.wait_ge(s_norm, t - 1)
                    if p == 0:
                        lin_free(0, 0)
                        lin_free(1, 0)
                    for w in range(2):
                        for hp in range(HP):
                            at = (p * HP + hp) * G * CP
                            i = nc.tensor.matmul(po[w * GP:w * GP + N, at:at + G * CP],
                                                 probs[p % 4][:, w * COLS + hp * N:w * COLS + (hp + 1) * N],
                                                 Vb[obar][:, (2 * p + w) * HP + hp, :], start=True, stop=True)
                    i.then_inc(s_pv, 1)

                def bias_pair(bank, table, ty, p, start):
                    dst = bank[0:AP_, 0:2 * COLS].rearrange("p (w n) -> p w n", w=2)
                    if p % 4 == 3:
                        src = table[:, ty:ty + 2, :]
                    else:
                        src = table[:, ty:ty + 1, :].to_broadcast([AP_, 2, COLS])
                    nc.tensor.matmul(dst, idt[0:AP_, 0:AP_], src, start=start, stop=False, skip_group_check=True)

                def scores(p):
                    bank = sc[p % 2]
                    if not (isinstance(t, int) and t == 0 and p < 2):
                        pe.wait_ge(s_max, PAIRS * t + p - 1)
                    bias_pair(bank, bs_h, 2 * edge, p, True)
                    for w in range(2):
                        for g in range(G):
                            i = nc.tensor.matmul(bank[g * GP:g * GP + N, w * COLS:(w + 1) * COLS],
                                                 Qd[par][0:KR, g, 2 * p + w, :], Kb[par][0:KR, g, :, 2 * p + w, :],
                                                 start=False, stop=True, skip_group_check=True)
                    i.then_inc(s_s, 1)

                if front:
                    pe.wait_ge(s_xT, t + 1)
                    qk_piece(0)
                if back:
                    pe.wait_ge(s_mrow, 16 * G * t)
                for p in range(PAIRS):
                    if back:
                        t_scores(p)
                    if front and p + 1 < 8:
                        qk_piece(p + 1)
                    if back and p > 0:
                        pv(p - 1)
                if front:
                    v_piece(0)
                    v_piece(1)
                if back:
                    pv(PAIRS - 1)

                def o_transposes():
                    pe.wait_ge(s_olo, t)
                    if front:
                        pe.wait_ge(s_xT, t + 1)
                    for p in range(PAIRS):
                        i = nc.tensor.transpose(psT[0:HL, p * 128:p * 128 + AP_], otok[:, p, :], idt[0:AP_, 0:AP_])
                    i.then_inc(s_otp, 1)

                def project():
                    pe.wait_ge(s_OT, t)
                    lin_free(0, 5 if front else 0)
                    flat = OT[:, :, :].rearrange("p w n -> p (w n)")
                    for c in range(CH):
                        tok = flat[:, c * PT:(c + 1) * PT]
                        dst = lin[0][0:PT, c * C:(c + 1) * C]
                        nc.tensor.matmul(dst, tok, wh[:, WP:WP + C], start=True, stop=False)
                        i = nc.tensor.matmul(dst, tok, wl[:, WP:WP + C], start=False, stop=True)
                    i.then_inc(s_qk[0], 1)

                if front:
                    pe.wait_ge(s_qk_ready, t + 1)
                for p in range(PAIRS):
                    if front:
                        scores(p)
                    if back and p == 3:
                        o_transposes()
                    if back and p == 5:
                        project()
                if front:
                    pe.wait_ge(s_m16, t + 1)
                    if back:
                        pe.wait_ge(s_OT, t)
                    nc.tensor.transpose(psT[0:MROW, 0:AP_], m16[:, :],
                                        idt[0:AP_, 0:AP_]).then_inc(s_mtp, 1)

            attention_phase(pe, step)

            def fc2(u, par):
                pe.wait_ge(s_g, 3 * u + 3)
                if not (isinstance(u, int) and u == 0):
                    pe.wait_ge(s_yo, u)
                for c in range(CH):
                    k, at = c // 4, (c % 4) * PT
                    dst = banks[6][0:PT, c * C:(c + 1) * C]
                    nc.tensor.matmul(dst, gel[par][:, k, at:at + PT], w2a[:, :], start=True, stop=False)
                    i = nc.tensor.matmul(dst, gel[par][:, 2, at:at + PT], w2b[:, k, :],
                                         start=False, stop=True)
                i.then_inc(s_y, 1)

            def unit(u, par, first):
                n = u + UNITS + 1
                if isinstance(u, int) and u == 0:
                    pe.wait_ge(s_linfree[0], used(0, UNITS) + 1)
                    pe.wait_ge(s_norm, UNITS)
                    pe.wait_ge(s_max, PAIRS * UNITS)
                pe.wait_ge(s_xT, n - 1)
                x_transposes(n)
                pe.wait_ge(s_xT, n)
                if not first:
                    pe.wait_ge(s_g, 3 * u - 3)
                for k in range(2):
                    lo, hi = (0, 4 * PT) if k == 0 else (4 * PT, TOK)
                    split_mm(banks[3 * par + k][:, 0:hi - lo], wh[:, WF1:WF1 + 128], wl[:, WF1:WF1 + 128],
                             xT[:, lo:hi]).then_inc(s_h, 1)
                for k in range(2):
                    lo, hi = (0, 4 * PT) if k == 0 else (4 * PT, TOK)
                    i = split_mm(banks[3 * par + 2][64 * k:64 * k + 64, 0:hi - lo], wh[:, WF1 + 128:WP],
                                 wl[:, WF1 + 128:WP], xT[:, lo:hi])
                i.then_inc(s_h, 1)
                if not (isinstance(u, int) and u == 0):
                    fc2(u - 1, 1 - par)
            mlp_phase(pe, unit)
            fc2(UNITS - 1, 1)

        @block.vector
        def _(dve):
            chain = [0]

            def link(i):
                chain[0] += 1
                i.then_inc(s_dve, 1)
                dve.wait_ge(s_dve, chain[0])

            for t in (*Qd, *Kd):
                nc.vector.memset(t[0:MROW, :, :, :], 0.0)
            for t in (*Qb, *Kb):
                for g in range(G):
                    nc.vector.memset(t[0:MROW, g, :, :, :], 0.0)
            for t in Kd:
                nc.vector.memset(t[MROW:MROW + 1, :, :, :], SM)
            nc.vector.memset(xtok[:, :, 2 * C:HL], SX)
            nc.vector.memset(otok[:, :, 2 * C:HL], SO)
            nc.vector.memset(m16[:, :], 0.0)
            for t in gel:
                nc.vector.memset(t[64:128, 2, 3 * PT:4 * PT], 0.0)
            nc.vector.memset(po[:, :], 1.0)
            dve.wait_ge(s_const, NCONST)
            dve.wait_ge(s_prep_p, 2)
            row = w32[2 * C:HL, :]
            link(nc.vector.tensor_tensor(row[:, 0:WF1], row[:, 0:WF1], lin[0][2 * C:HL, 0:WF1], ALU.add))
            link(nc.vector.tensor_tensor(row[:, WF1:WP], row[:, WF1:WP], lin[1][2 * C:HL, 0:HID], ALU.add))
            link(nc.vector.tensor_scalar(w32[0:2 * C, 0:WF1], w32[0:2 * C, 0:WF1], gain[:, 0:1], None, ALU.mult))
            link(nc.vector.tensor_scalar(w32[0:2 * C, WF1:WP], w32[0:2 * C, WF1:WP], gain[:, 1:2], None, ALU.mult))
            link(nc.vector.tensor_scalar(w32[:, 0:WK[0]], w32[:, 0:WK[0]], float(HD ** -0.5), None, ALU.mult))
            link(nc.vector.tensor_scalar(wh[:, :], w32[:, :], SWT, None, ALU.mult))
            link(nc.vector.scalar_tensor_tensor(wl[:, :], w32[:, :], SWT, wh[:, :], ALU.mult, ALU.subtract))
            for k, (hi, lo) in enumerate(((bs_h, None), (bt_h, bt_l))):
                link(nc.vector.tensor_tensor(biasr[:, :, :], mask32[:, :, :],
                                             rpb32[:, k:k + 1, :].to_broadcast([AP_, 4, COLS]), ALU.add))
                link(nc.vector.tensor_scalar(hi[:, :, :], biasr[:, :, :], SB, None, ALU.mult))
                if lo is not None:
                    f = "p a n -> p (a n)"
                    link(nc.vector.scalar_tensor_tensor(lo[:, :, :].rearrange(f), biasr[:, :, :].rearrange(f), SB,
                                                        hi[:, :, :].rearrange(f), ALU.mult, ALU.subtract))
            nc.vector.memset(nmean[:, :], 0.0).then_inc(s_prep, 1)
            base = chain[0]

            def mean(u, n):
                nc.vector.tensor_reduce(ssum[:, :], x_of(u), AX.X, ALU.add).then_inc(s_dve, 1)
                dve.wait_ge(s_dve, base + 2 * n - 1)
                nc.vector.tensor_scalar(nmean[:, :], ssum[:, :], -1.0 / C, None, ALU.mult).then_inc(s_mean, 1)

            def variance(n):
                dve.wait_ge(s_sq, n)
                nc.vector.tensor_reduce(ssum[:, :], sq[:, :, :], AX.X, ALU.add).then_inc(s_dve, 1)
                dve.wait_ge(s_dve, base + 2 * n)
                nc.vector.tensor_scalar(var[:, :], ssum[:, :], 1.0 / C, EPS, ALU.mult, ALU.add).then_inc(s_var, 1)

            def x_low(n):
                dve.wait_ge(s_xhi, n)
                nc.vector.scalar_tensor_tensor(xtok[:, :, C:2 * C], xn[:, :, :], SX, xtok[:, :, 0:C],
                                               ALU.mult, ALU.subtract).then_inc(s_xlo, 1)

            def step(dve, t, par, edge, edge_b, first, last):
                front, back = not last, not first
                nxt = front and not (isinstance(t, int) and t >= UNITS - 1)
                if first:
                    dve.wait_ge(s_x[0], 16)
                    mean(0, 1)
                    variance(1)
                    x_low(1)
                if nxt:
                    dve.wait_ge(s_x[1 - par], 8 * (t + par) + 16)
                    mean(t + 1, t + 2)

                def qk_low(j):
                    ten, isq, g, half, b = (Kd, Qd)[j // 2 % 2][par], j // 2 % 2, j // 4, j % 2, j % 2
                    r = KQ if isq else 2 * KQ
                    dve.wait_ge(s_qkh, 8 * t + j + 1)
                    part = ten[r:r + KD, g, half * 8:half * 8 + 8, :].rearrange("p w n -> p (w n)")
                    nc.vector.scalar_tensor_tensor(part, lin[b][r:r + KD, 0:HALF], SQ / (SX * SWT), part,
                                                   ALU.mult, ALU.subtract).then_inc(s_linfree[b], 1)
                    if half == 1:
                        for k in range(2):
                            dve.wait_ge(s_linfree[k], used(k, t) + j // 2 + 1)
                        dst = (Kb, Qb)[isq][par]
                        for hp in range(HP):
                            i = nc.vector.tensor_scalar(dst[0:KR, g, hp, :, :].rearrange("p w n -> p (w n)"),
                                                        ten[0:KR, g, :, :].rearrange("p w n -> p (w n)"),
                                                        headrow[:, hp:hp + 1], None, ALU.mult)
                        if j == 7:
                            i.then_inc(s_qk_ready, 1)

                if front:
                    for j in range(8):
                        qk_low(j)
                        if j == 5 and nxt:
                            variance(t + 2)
                if back:
                    dve.wait_ge(s_pv, PAIRS * t)
                    o = po[0:AP_, 0:PAIRS * NH * CP].rearrange("p (a d) -> p a d", d=CP)
                    nc.vector.reciprocal(rsum[:, :], o[:, :, HD]).then_inc(s_rsum, 1)
                    dve.wait_ge(s_rsum, t)
                    nc.vector.tensor_tensor(on[:, :, :].rearrange("p a (h d) -> p (a h) d", d=HD), o[:, :, 0:HD],
                                            rsum[:, :].unsqueeze(2).to_broadcast([AP_, PAIRS * NH, HD]),
                                            ALU.mult).then_inc(s_norm, 1)
                for p in range(PAIRS):
                    if front:
                        dve.wait_ge(s_s, PAIRS * t + p + 1)
                        nc.vector.tensor_reduce(rowmax[:, 2 * p:2 * p + 2, :],
                                                sc[p % 2][0:AP_, 0:2 * COLS].rearrange("p (a n) -> p a n", n=N),
                                                AX.X, ALU.max).then_inc(s_max, 1)
                    if back and p == 1:
                        dve.wait_ge(s_ohi, t)
                        nc.vector.scalar_tensor_tensor(otok[:, :, C:2 * C], on[:, :, :], SO, otok[:, :, 0:C],
                                                       ALU.mult, ALU.subtract).then_inc(s_olo, 1)
                    if back and p == 6:
                        dve.wait_ge(s_qk[0], used(0, t) + (6 if front else 1))
                        y = lin[0][0:PT, 0:CH * C].rearrange("p (c n) -> p c n", n=C)
                        nc.vector.scalar_tensor_tensor(x_of(t - 1), y, 1.0 / (SO * SWT), x_of(t - 1),
                                                       ALU.mult, ALU.add).then_inc(s_linfree[0], 1)
                    if nxt and p == 4:
                        x_low(t + 2)
                if front:
                    dve.wait_ge(s_max, PAIRS * (t + 1))
                    nc.vector.tensor_scalar(m16[:, 0:HP * UW].rearrange("p (a w) -> p a w", a=HP), rowmax[:, :, :].rearrange("p w a -> p a w"), -1.0 / SM, None,
                                            ALU.mult).then_inc(s_m16, 1)
                    dve.wait_ge(s_mtp, t + 1)
                    if back:
                        dve.wait_ge(s_mrow, 16 * G * t)
                    nc.vector.tensor_copy(mT[:, :], psT[0:HP * UW, 0:AP_]).then_inc(s_mT, 1)
            attention_phase(dve, step)

            dve.wait_ge(s_linfree[0], used(0, UNITS) + 1)

            def unit(u, par, first):
                n = u + UNITS + 1
                mean(u, n)
                variance(n)
                x_low(n)
                if not (isinstance(u, int) and u == 0):
                    finish(u - 1, 1 - par, first)

            def finish(u, par, first):
                dve.wait_ge(s_y, u + 1)
                dve.wait_ge(s_x1b, u + 1)
                if not (isinstance(u, int) and u < 2):
                    dve.wait_ge(s_store[par], 8 * (u - par))
                nc.vector.tensor_tensor(ybuf[par][:, :].rearrange("p (c n) -> p c n", n=C),
                                        banks[6][0:PT, 0:CH * C].rearrange("p (c n) -> p c n", n=C), x_of(u),
                                        ALU.add).then_inc(s_yo, 1)
            mlp_phase(dve, unit)
            finish(UNITS - 1, 1, False)


def _windows(x):
    x = np.roll(x, (-SS, -SS), axis=(1, 2)).reshape(B, H // WS, WS, NWX, WS, C)
    x = x.transpose(1, 0, 3, 2, 4, 5).reshape(UNITS, CH, PT, C)
    return np.ascontiguousarray(x.transpose(0, 2, 1, 3)).reshape(UNITS, PT, CH * C)


def _image(y):
    y = y.reshape(UNITS, PT, CH, C).transpose(0, 2, 1, 3).reshape(H // WS, B, NWX, WS, WS, C)
    y = y.transpose(1, 0, 3, 2, 4, 5).reshape(B, H, W, C)
    return np.ascontiguousarray(np.roll(y, (SS, SS), axis=(1, 2)))


def _weights(qkv_w, qkv_b, proj_w, proj_b, fc1_w, fc1_b):
    def stack(w, b):
        return np.concatenate([w, w, b[None]], axis=0)

    qkv = stack(qkv_w, qkv_b)
    w = np.zeros((HL, WCOLS), np.float32)
    for g in range(G):
        for k, at in enumerate((WQ[g], WK[g])):
            cols = qkv[:, k * C:(k + 1) * C].reshape(HL, HP, G, HD)[:, :, g, :].reshape(HL, KD)
            for r in range(3):
                w[:, at + r * KQ:at + r * KQ + KD] = cols
    w[:, WV:WV + C] = qkv[:, 2 * C:3 * C]
    w[:, WF1:WF1 + HID] = stack(fc1_w, fc1_b)
    w[:, WP:WP + C] = stack(proj_w, proj_b)
    return w


def _position_bias(table):
    i = np.arange(N)
    r, c = i // WS, i % WS
    at = (r[:, None] - r[None, :] + WS - 1) * (2 * WS - 1) + (c[:, None] - c[None, :] + WS - 1)
    out = np.zeros((AP_, 2, HP, N), np.float32)
    for g in range(G):
        for hp in range(HP):
            m = table[:, 2 * hp + g][at]
            out[g * GP:g * GP + N, 0, hp] = m
            out[g * GP:g * GP + N, 1, hp] = m.T
    return out.reshape(AP_, 2, COLS)


def _window_mask():
    out = np.zeros((AP_, 4, HP, N), np.float32)
    i = np.arange(N)
    for kind in range(4):
        row = (i // WS >= WS - SS) if kind // 2 else np.zeros(N, bool)
        col = (i % WS >= WS - SS) if kind % 2 else np.zeros(N, bool)
        region = 2 * row + col
        m = np.where(region[:, None] != region[None, :], -100.0, 0.0)
        for g in range(G):
            out[g * GP:g * GP + N, kind] = m[:, None, :]
    return out.reshape(AP_, 4, COLS)


def kernel(**inputs):
    import concourse.bacc as bacc
    from concourse.bass_utils import run_bass_kernel_spmd

    p = {k.replace("L0_conv_", ""): np.asarray(v) for k, v in inputs.items()}
    shifts = np.zeros((C, 2, HL), np.float32)
    shifts[:, 0, 2 * C] = p["norm1_b"]
    shifts[:, 1, 2 * C] = p["norm2_b"]
    gains = np.stack([np.concatenate([p[k]] * 2) for k in ("norm1_g", "norm2_g")], axis=1)
    headrow = np.zeros((KR, HP), np.float32)
    for r in range(3):
        for hp in range(HP):
            headrow[r * KQ + hp * HD:r * KQ + (hp + 1) * HD, hp] = 1.0
    w2 = np.zeros((128, 3, C), np.float32)
    w2[:, 0] = p["fc2_w"][0:128]
    for k in range(2):
        w2[64 * k:64 * k + 64, 1 + k] = p["fc2_w"][128:HID]
    onescol = np.zeros((AP_, UW * HP, G, CP), np.float32)
    for g in range(G):
        onescol[g * GP:g * GP + N, :, g, HD] = 1.0
    arrays = {
        "x": _windows(p["x"]),
        "weights": _weights(p["qkv_w"], p["qkv_b"], p["proj_w"], p["proj_b"], p["fc1_w"], p["fc1_b"]),
        "gains": gains,
        "shifts": shifts,
        "w2": w2,
        "b2": np.ascontiguousarray(np.broadcast_to(p["fc2_b"], (PT, C))),
        "rpb": _position_bias(p["rpb_table"]),
        "headrow": headrow,
        "maskt": _window_mask(),
        "ident": np.eye(128, dtype=np.float16),
        "onescol": onescol.reshape(AP_, UW * HP, G * CP),
    }
    nc = bacc.Bacc("TRN2", target_bir_lowering=False, num_devices=1)
    args = [nc.dram_tensor(f"in_{k}", a.shape, mybir.dt.from_np(a.dtype), kind="ExternalInput").ap()
            for k, a in arrays.items()]
    out = nc.dram_tensor("out_y", (UNITS, PT, CH * C), mybir.dt.float32, kind="ExternalOutput").ap()
    swin_block_kernel(nc, *args, out)
    r = run_bass_kernel_spmd(nc, [{f"in_{k}": a for k, a in arrays.items()}], core_ids=[0])
    return _image(r.results[0]["out_y"])
```

```python
import numpy as np
import concourse.bass as bass
from concourse import mybir
from contextlib import ExitStack

B, H, W, C = 16, 56, 56, 48
WS, SS, NH = 7, 3, 6
N = WS * WS
HD = C // NH
HID = 4 * C
NWX = W // WS
EPS = 1e-5

UW = 16
UNITS = B * (H // WS) * NWX // UW
EDGE = UNITS - UNITS // (H // WS)
TOK = UW * N
CH = 7
PT = TOK // CH
HALF = TOK // 2
PAIRS = UW // 2
G, HP = 2, 3
GP = 64
AP_ = GP + N
FULL = 128
KQ = 32
KD = HP * HD
MROW = KQ + KD
HL = 2 * C + 1
COLS = HP * N
CP = HD + 1

SX, SWT = 4096.0, 64.0
SQ = 16.0
SB = SQ * SQ
SM = 4096.0
SV = 64.0
SO = 256.0
SG = 16.0
LOGP = 8 * float(np.log(2.0))

WQ = 0
WK = FULL
WV = 2 * FULL
WF1 = WV + C
WF1B = WF1 + FULL
WP = WF1B + 2 * FULL
WCOLS = WP + C
HTOK = 4 * PT

TLAG = 3
PLAG = 5
GW = HTOK + FULL - PT


def exists(u):
    return not isinstance(u, int) or 0 <= u < UNITS


def done(u):
    return min(max(u + 1, 0), UNITS) if isinstance(u, int) else u + 1


def wait(engine, semaphore, value):
    if not (isinstance(value, int) and value <= 0):
        engine.wait_ge(semaphore, value)


def t_pair(t, slot):
    return (t - 1, slot - TLAG) if slot >= TLAG else (t - 2, slot - TLAG + PAIRS)


def v_pair(t, slot):
    return (t - 1, slot - PLAG) if slot >= PLAG else (t - 2, slot - PLAG + PAIRS)


def lin_at(t, k):
    if not isinstance(t, int):
        return 6 * t + 1 + k
    return (4 * done(t) + (min(k, 4) if exists(t + 1) else 0) + done(t - 4) + (1 if k > 4 and exists(t - 3) else 0)
            + done(t - 1) + (1 if k > 5 and exists(t) else 0))


def swin_block_kernel(nc, x, weights, gains, shifts, w2, b2, rpb, headrow_d, grow_d, maskt, ident, onescol, out):
    f32, f16 = mybir.dt.float32, mybir.dt.float16
    ALU, ACT, AX = mybir.AluOpType, mybir.ActivationFunctionType, mybir.AxisListType
    ctx = ExitStack()
    with ctx:
        def sb(name, shape, dt, within=ctx):
            return within.enter_context(nc.sbuf_tensor(name, shape, dt))

        def sem(name):
            return ctx.enter_context(nc.semaphore(name))

        xres = sb("xres", [PT, UNITS, CH * C], f32)
        nmean = sb("nmean", [PT, CH], f32)
        xc = sb("xc", [PT, CH, C], f32)
        sq = sb("sq", [PT, CH, C], f32)
        ssum = sb("ssum", [PT, CH], f32)
        var = sb("var", [PT, CH], f32)
        rstd = sb("rstd", [PT, CH], f32)
        mhalf = sb("mhalf", [PT, CH], f32)
        xn = sb("xn", [PT, CH, C], f32)
        xtok = sb("xtok", [PT, CH, FULL], f16)
        wh = sb("wh", [HL, WCOLS], f16)
        wl = sb("wl", [HL, WCOLS], f16)
        w2h = sb("w2h", [128, 3, C], f16)
        w2l = sb("w2l", [128, 3, C], f16)
        b2t = sb("b2t", [PT, C], f32)
        idt = sb("idt", [FULL, FULL], f16)

        banks = [ctx.enter_context(nc.psum_tensor(f"bank{i}", [128, 512], f32)) for i in range(7)]
        psT = ctx.enter_context(nc.psum_tensor("psT", [128, 1024], f16))
        lin, sc, st, po = banks[0], banks[1:3], banks[3:5], banks[5:7]

        s_x = [sem(f"x_loaded{i}") for i in range(2)]
        s_const = sem("constants_loaded")
        s_prep = sem("weights_prepared")
        s_prep_p = sem("shift_products")
        s_link = sem("preparation_chain")
        s_sum = sem("sums_ready")
        s_mean = sem("mean_ready")
        s_xc = sem("centred")
        s_sq = sem("squared")
        s_var = sem("variance_ready")
        s_pow = sem("rstd_ready")
        s_xn = sem("normalized")
        s_xhi = sem("x_high_ready")
        s_xlo = sem("x_low_ready")
        s_xtp = sem("x_transposed")
        s_xT = sem("xT_ready")
        s_lin = sem("lin_full")
        s_linfree = sem("lin_free")
        s_high = sem("qk_high_ready")
        s_vhigh = sem("v_high_ready")
        s_sb = sem("score_operands_ready")
        s_tb = sem("tscore_operands_ready")
        s_qbh = sem("q_low_blocks_ready")
        s_s = sem("scores_full")
        s_max = sem("rowmax_ready")
        s_m16 = sem("m16_ready")
        s_mtp = sem("m_transposed")
        s_mT = sem("mT_ready")
        s_mrow = sem("m_rows_written")
        s_st = sem("tscores_full")
        s_exp = sem("probs_ready")
        s_pl = sem("probs_low_ready")
        s_pv = sem("pv_done")
        s_rsum = sem("rsum_ready")
        s_norm = sem("attention_normalized")
        s_ohi = sem("o_high_ready")
        s_olo = sem("o_low_ready")
        s_otp = sem("o_transposed")
        s_OT = sem("OT_ready")
        s_pads = sem("mlp_pads_ready")
        s_h = sem("hidden_full")
        s_g = sem("gelu_ready")
        s_gs = sem("gelu_high_ready")
        s_gl = sem("gelu_low_ready")
        s_x1b = sem("x1_with_bias")
        s_y = sem("y_full")
        s_yo = sem("y_ready")
        s_store = [sem(f"stored{i}") for i in range(2)]

        NCONST = 16 * 14

        def x_of(u):
            return xres[:, bass.ds(u, 1), :].rearrange("p u (c n) -> p (u c) n", n=C)

        def ln_mean(dve, u, n):
            nc.vector.tensor_reduce(ssum[:, :], x_of(u), AX.X, ALU.add).then_inc(s_sum, 1)
            dve.wait_ge(s_sum, 2 * n - 1)
            nc.vector.tensor_scalar(nmean[:, :], ssum[:, :], -1.0 / C, None, ALU.mult).then_inc(s_mean, 1)

        def ln_centre(pool, u, n):
            pool.wait_ge(s_mean, n)
            nc.gpsimd.tensor_tensor(xc[:, :, :], x_of(u), nmean[:, :].unsqueeze(2).to_broadcast([PT, CH, C]),
                                    ALU.add).then_inc(s_xc, 1)

        def ln_square(act, n):
            act.wait_ge(s_xc, n)
            nc.scalar.activation(sq[:, :, :], xc[:, :, :], ACT.Square).then_inc(s_sq, 1)

        def ln_variance(dve, n):
            dve.wait_ge(s_sq, n)
            nc.vector.tensor_reduce(ssum[:, :], sq[:, :, :], AX.X, ALU.add).then_inc(s_sum, 1)
            dve.wait_ge(s_sum, 2 * n)
            nc.vector.tensor_scalar(var[:, :], ssum[:, :], 1.0 / C, EPS, ALU.mult, ALU.add).then_inc(s_var, 1)

        def ln_rsqrt(pool, n):
            pool.wait_ge(s_var, n)
            nc.gpsimd.tensor_tensor(rstd[:, :], var[:, :], mhalf[:, :], ALU.pow).then_inc(s_pow, 1)

        def ln_scale(pool, n):
            pool.wait_ge(s_pow, n + 1)
            nc.gpsimd.tensor_tensor(xn[:, :, :], xc[:, :, :], rstd[:, :].unsqueeze(2).to_broadcast([PT, CH, C]),
                                    ALU.mult).then_inc(s_xn, 1)

        def ln_high(act, n):
            act.wait_ge(s_xn, n)
            wait(act, s_xtp, n - 1)
            nc.scalar.activation(xtok[:, :, 0:C], xn[:, :, :], ACT.Copy, scale=SX).then_inc(s_xhi, 1)

        def ln_low(dve, n):
            dve.wait_ge(s_xhi, n)
            nc.vector.scalar_tensor_tensor(xtok[:, :, C:2 * C], xn[:, :, :], SX, xtok[:, :, 0:C],
                                           ALU.mult, ALU.subtract).then_inc(s_xlo, 1)

        def x_transposes(pe, n):
            pe.wait_ge(s_xlo, n)
            for c in range(CH):
                i = nc.tensor.transpose(psT[:, c * PT:(c + 1) * PT], xtok[:, c, :], idt[0:PT, 0:PT])
            i.then_inc(s_xtp, 1)

        actx = ExitStack()
        ctx.enter_context(actx)

        def sba(name, shape, dt):
            return sb(name, shape, dt, actx)

        w32 = sba("w32", [HL, WCOLS], f32)
        gain = sba("gain", [2 * C, 2], f32)
        shift = sba("shift", [C, 2, HL], f32)
        w2f = sba("w2f", [128, 3, C], f32)
        rpb32 = sba("rpb32", [AP_, 2, COLS], f32)
        mask32 = sba("mask32", [AP_, 4, COLS], f32)
        bs_h = sba("bs_h", [AP_, 4, COLS], f16)
        bt_h = sba("bt_h", [AP_, 4, COLS], f16)
        bt_l = sba("bt_l", [AP_, 4, COLS], f16)
        headrow = sba("headrow", [FULL, HP], f32)
        grow = sba("grow", [FULL, G], f32)
        xT = [sba(f"xT{i}", [HL, UW, GP], f16) for i in range(2)]
        QA = [sba(f"QA{i}", [FULL, UW, N], f16) for i in range(2)]
        KA = [sba(f"KA{i}", [FULL, UW, N], f16) for i in range(2)]
        QB = [sba(f"QB{i}", [FULL, UW, N], f16) for i in range(2)]
        QAg = [sba(f"QAg{i}", [FULL, UW, G, GP], f16) for i in range(2)]
        KAh = [sba(f"KAh{i}", [FULL, HP, UW, N], f16) for i in range(2)]
        KAg = [sba(f"KAg{i}", [FULL, UW, G, GP], f16) for i in range(2)]
        QAh = [sba(f"QAh{i}", [FULL, HP, UW, N], f16) for i in range(2)]
        QBh = [sba(f"QBh{i}", [FULL, HP, UW, N], f16) for i in range(2)]
        Vh = [sba(f"Vh{i}", [AP_, 2, PAIRS, HP, G * CP], f16) for i in range(2)]
        Vl = [sba(f"Vl{i}", [AP_, 2, PAIRS, HP, G * CP], f16) for i in range(2)]
        rowmax = sba("rowmax", [AP_, UW, HP], f32)
        m16 = sba("m16", [AP_, FULL], f16)
        mT = sba("mT", [HP * UW, AP_], f16)
        p32 = [sba(f"p32_{i}", [AP_, 2, HP, N], f32) for i in range(4)]
        ph = [sba(f"ph{i}", [AP_, HP, 2, GP], f16) for i in range(4)]
        pl = [sba(f"pl{i}", [AP_, HP, 2, GP], f16) for i in range(4)]
        rsum = sba("rsum", [AP_, 2, 4 * HP * 2 * G], f32)
        on = sba("on", [AP_, PAIRS, C], f32)
        otok = sba("otok", [AP_, PAIRS, FULL], f16)
        OT = sba("OT", [HL, TOK + FULL - PT], f16)

        def v_src(w, g):
            return lin[w * GP:w * GP + N, 0:PAIRS * C].rearrange("p (a g d) -> p a g d", g=G, d=HD)[:, :, g, :]

        def v_dst(V, par, w, g):
            return V[par][g * GP:g * GP + N, w, :, :, g * CP:g * CP + HD].rearrange("p a h d -> p (a h) d")

        def attention_phase(e, step):
            for t in range(-2, TLAG):
                step(t, t % 2, False)
            with e.Fori(3, EDGE - 2, 2) as i:
                step(i, 1, False)
                step(i + 1, 0, False)
            for t in range(EDGE - 1, EDGE + 2):
                step(t, t % 2, False)
            with e.Fori(EDGE + 2, UNITS - 3, 2) as i:
                step(i, 0, True)
                step(i + 1, 1, True)
            for t in range(UNITS - 2, UNITS + 3):
                step(t, t % 2, True)

        def wrapped(u, late):
            return u >= EDGE if isinstance(u, int) else late

        block = actx.enter_context(nc.Block())

        @block.sync
        def _(sp):
            for dst, src in ((w32, weights), (gain, gains), (shift, shifts), (w2f, w2), (b2t, b2), (rpb32, rpb),
                             (mask32, maskt), (idt, ident), (headrow, headrow_d), (grow, grow_d), (Vh[0], onescol[0]),
                             (Vh[1], onescol[0]), (Vl[0], onescol[1]), (Vl[1], onescol[1])):
                sp.dma_start(dst[:], src).then_inc(s_const, 16)

            def load(u, par):
                wait(sp, s_x[par], 8 * (u - par))
                sp.dma_start(xres[:, bass.ds(u, 1), :], x[bass.ds(u, 1), :, :].rearrange("u p n -> p u n")).then_inc(s_x[par], 16)
            for u in range(3):
                load(u, u % 2)

            def step(t, par, late):
                if exists(t + 5) and not late:
                    load(t + 5, 1 - par)
                if isinstance(t, int) and t == EDGE + 1:
                    load(t + 6, par)
                if exists(t - 1):
                    sp.wait_ge(s_mT, done(t - 1))
                    sp.wait_ge(s_qbh, done(t - 1))
                    for g in range(G):
                        sp.dma_start(QBh[1 - par][MROW + g:MROW + g + 1, :, :, :].rearrange("o a w n -> o (a w) n"),
                                     mT[:, g * GP:g * GP + N]).then_inc(s_mrow, 16)
            attention_phase(sp, step)

        @block.gpsimd
        def _(pool):
            nc.gpsimd.memset(mhalf[:, :], -0.5).then_inc(s_pow, 1)
            pool.wait_ge(s_pow, 1)
            pool.wait_ge(s_prep, 1)

            def step(t, par, late):
                def low(u, p):
                    pool.wait_ge(s_exp, PAIRS * u + p + 1)
                    nc.gpsimd.tensor_tensor(pl[p % 4][:, :, :, 0:N].rearrange("p a w n -> p w a n"), p32[p % 4][:, :, :, :],
                                            ph[p % 4][:, :, :, 0:N].rearrange("p a w n -> p w a n"),
                                            ALU.subtract).then_inc(s_pl, 1)

                for s in range(PAIRS):
                    u, p = t_pair(t, s)
                    if exists(u):
                        low(u, p)
                    if exists(t + 2):
                        if s == 1:
                            ln_centre(pool, t + 2, t + 3)
                        if s == 3:
                            ln_rsqrt(pool, t + 3)
                        if s == 4:
                            ln_scale(pool, t + 3)
                    if exists(t) and s >= 5:
                        hp = s - 5
                        dst, src = QBh[par][:, hp, :, :], QB[par]
                        lo = 0
                        if hp == 0:
                            pool.wait_ge(s_linfree, lin_at(t, 0))
                            nc.gpsimd.tensor_tensor(dst[:, 0, :], src[:, 0, :], headrow[:, 0:1].to_broadcast([FULL, N]),
                                                    ALU.mult)
                            lo = 1
                        i = nc.gpsimd.tensor_scalar(dst[:, lo:UW, :].rearrange("p w n -> p (w n)"),
                                                    src[:, lo:UW, :].rearrange("p w n -> p (w n)"),
                                                    headrow[:, hp:hp + 1], 1.0, ALU.mult, ALU.mult)
                        if hp == HP - 1:
                            i.then_inc(s_qbh, 1)
            attention_phase(pool, step)

        @block.scalar
        def _(act):
            act.wait_ge(s_prep, 1)

            def step(t, par, late):
                def qk_high(j):
                    dst = (KA, QA)[j // 2][1 - par][:, 8 * (j % 2):8 * (j % 2) + 8, :].rearrange("p w n -> p (w n)")
                    act.wait_ge(s_lin, lin_at(t, j) + 1)
                    if j == 0:
                        wait(act, s_tb, done(t - 1))
                    nc.scalar.activation(dst, lin[:, 0:HALF], ACT.Copy, scale=SQ / (SX * SWT)).then_inc(s_high, 1)

                def v_high():
                    act.wait_ge(s_lin, lin_at(t, 5) + 1)
                    wait(act, s_pv, PAIRS * done(t - 2))
                    for w in range(2):
                        for g in range(G):
                            i = nc.scalar.activation(v_dst(Vh, par, w, g), v_src(w, g), ACT.Copy, scale=SV / (SX * SWT))
                    i.then_inc(s_vhigh, 1)

                def exp(u, p):
                    act.wait_ge(s_st, PAIRS * u + p + 1)
                    wait(act, s_pv, PAIRS * u + p - 3)
                    src = st[p % 2][0:AP_, 0:2 * COLS].rearrange("p (w a n) -> p w a n", w=2, n=N)
                    nc.scalar.activation(ph[p % 4][:, :, :, 0:N].rearrange("p a w n -> p w a n"), src, ACT.Exp,
                                         scale=1.0 / SB)
                    nc.scalar.activation(p32[p % 4][:, :, :, :], src, ACT.Exp, scale=1.0 / SB).then_inc(s_exp, 1)

                for s in range(PAIRS):
                    if exists(t + 1) and s < 4:
                        qk_high(s)
                    if exists(t) and s == 6:
                        v_high()
                    u, p = t_pair(t, s)
                    if exists(u):
                        exp(u, p)
                    if exists(t - 3) and s == 1:
                        act.wait_ge(s_otp, done(t - 3))
                        nc.scalar.activation(OT[:, 0:TOK].rearrange("p (w n) -> p w n", n=N),
                                             psT[0:HL, :].rearrange("p (w n) -> p w n", n=GP)[:, :, 0:N],
                                             ACT.Copy).then_inc(s_OT, 1)
                    if exists(t + 2) and s == 2:
                        ln_square(act, t + 3)
                    if exists(t + 2) and s == 5:
                        ln_high(act, t + 3)
                    if exists(t - 2) and s == 6:
                        act.wait_ge(s_norm, 2 * done(t - 2))
                        nc.scalar.activation(otok[:, :, 0:C], on[:, :, :], ACT.Copy).then_inc(s_ohi, 1)
                    if exists(t + 2) and s == 7:
                        act.wait_ge(s_xtp, done(t + 2))
                        nc.scalar.activation(xT[par][:, :, 0:N], psT[0:HL, 0:TOK].rearrange("p (w n) -> p w n", n=N),
                                             ACT.Copy).then_inc(s_xT, 1)
            attention_phase(act, step)

        @block.tensor
        def _(pe):
            pe.wait_ge(s_const, NCONST)
            nc.tensor.matmul(banks[0][0:HL, 0:WF1], shift[:, 0, :], w32[0:C, 0:WF1], start=True, stop=True).then_inc(s_prep_p, 1)
            nc.tensor.matmul(banks[1][0:HL, 0:WP - WF1], shift[:, 1, :], w32[0:C, WF1:WP], start=True, stop=True)\
              .then_inc(s_prep_p, 1)
            pe.wait_ge(s_prep, 1)

            def step(t, par, late):
                def lin_free(k):
                    wait(pe, s_linfree, lin_at(t, k))

                def qk_piece(j):
                    col = (WK, WQ)[j // 2]
                    if j == 0:
                        pe.wait_ge(s_xT, done(t + 1))
                    lin_free(j)
                    tok = xT[1 - par][:, 8 * (j % 2):8 * (j % 2) + 8, 0:N]
                    nc.tensor.matmul(lin[:, 0:HALF], wh[:, col:col + FULL], tok, start=True, stop=False)
                    nc.tensor.matmul(lin[:, 0:HALF], wl[:, col:col + FULL], tok, start=False, stop=True).then_inc(s_lin, 1)

                def v_piece():
                    lin_free(5)
                    for p in range(PAIRS):
                        tok = xT[par][:, 2 * p:2 * p + 2, :].rearrange("p w n -> p (w n)")
                        dst = lin[:, p * C:(p + 1) * C]
                        nc.tensor.matmul(dst, tok, wh[:, WV:WV + C], start=True, stop=False)
                        i = nc.tensor.matmul(dst, tok, wl[:, WV:WV + C], start=False, stop=True)
                    i.then_inc(s_lin, 1)

                def bias_pair(bank, table, in_last_strip, p, start):
                    kind = 2 * in_last_strip
                    if p % 4 == 3:
                        src = table[:, kind:kind + 2, :]
                    else:
                        src = table[:, kind:kind + 1, :].to_broadcast([AP_, 2, COLS])
                    nc.tensor.matmul(bank[:, 0:2 * COLS].rearrange("p (w n) -> p w n", w=2), idt[0:AP_, :], src,
                                     start=start, stop=False, skip_group_check=True)

                def scores(p):
                    bank = sc[p % 2]
                    if p == 0:
                        pe.wait_ge(s_sb, done(t))
                    wait(pe, s_max, PAIRS * t + p - 1)
                    bias_pair(bank, bs_h, wrapped(t, late), p, True)
                    for w in range(2):
                        i = nc.tensor.matmul(bank[:, w * COLS:(w + 1) * COLS],
                                             QAg[par][:, 2 * p + w, :, :].rearrange("p g n -> p (g n)"),
                                             KAh[par][:, :, 2 * p + w, :], start=False, stop=True, skip_group_check=True)
                    i.then_inc(s_s, 1)

                def t_scores(u, upar, p):
                    bank = st[p % 2]
                    if p == 0:
                        pe.wait_ge(s_tb, done(u))
                        pe.wait_ge(s_mrow, 16 * G * done(u))
                    wait(pe, s_exp, PAIRS * u + p - 1)
                    bias_pair(bank, bt_h, wrapped(u, late), p, True)
                    bias_pair(bank, bt_l, wrapped(u, late), p, False)
                    for w in range(2):
                        for q in (QAh, QBh):
                            i = nc.tensor.matmul(bank[:, w * COLS:(w + 1) * COLS],
                                                 KAg[upar][:, 2 * p + w, :, :].rearrange("p g n -> p (g n)"),
                                                 q[upar][:, :, 2 * p + w, :], start=False, stop=True, skip_group_check=True)
                    i.then_inc(s_st, 1)

                def pv(u, upar, p):
                    pe.wait_ge(s_pl, PAIRS * u + p + 1)
                    if p == 0:
                        pe.wait_ge(s_linfree, lin_at(t, 0))
                    if p % 4 == 0:
                        wait(pe, s_norm, 2 * (u - 1) + p // 4 + 1)
                    for hp in range(HP):
                        at = (p % 4 * HP + hp) * 2 * G * CP
                        dst = po[p // 4][:, at:at + 2 * G * CP].rearrange("p (w n) -> p w n", w=2)
                        for k, (pr, v) in enumerate(((ph, Vh), (ph, Vl), (pl, Vh))):
                            i = nc.tensor.matmul(dst, pr[p % 4][:, hp, :, :].rearrange("p w n -> p (w n)"),
                                                 v[upar][:, :, p, hp, :], start=(k == 0), stop=(k == 2))
                    i.then_inc(s_pv, 1)

                for s in range(PAIRS):
                    if exists(t):
                        scores(s)
                    if exists(t + 1) and s < 4:
                        qk_piece(s)
                    u, p = t_pair(t, s)
                    if exists(u):
                        t_scores(u, 1 - par if s >= TLAG else par, p)
                    if exists(t - 1) and s == 0:
                        pe.wait_ge(s_m16, done(t - 1))
                        pe.wait_ge(s_xT, done(t + 1))
                        nc.tensor.transpose(psT[:, 0:AP_], m16[:, :], idt[0:AP_, 0:AP_]).then_inc(s_mtp, 1)
                    if exists(t - 3) and s == 1:
                        pe.wait_ge(s_olo, done(t - 3))
                        pe.wait_ge(s_mT, done(t - 1))
                        for k in range(PAIRS):
                            i = nc.tensor.transpose(psT[:, k * FULL:k * FULL + AP_], otok[:, k, :], idt[0:AP_, 0:AP_])
                        i.then_inc(s_otp, 1)
                    u, p = v_pair(t, s)
                    if exists(u):
                        pv(u, 1 - par if s >= PLAG else par, p)
                    if exists(t - 3) and s == 4:
                        pe.wait_ge(s_OT, done(t - 3))
                        lin_free(4)
                        for c in range(CH):
                            tok = OT[:, c * PT:c * PT + FULL]
                            dst = lin[:, c * C:(c + 1) * C]
                            nc.tensor.matmul(dst, tok, wh[:, WP:WP + C], start=True, stop=False)
                            i = nc.tensor.matmul(dst, tok, wl[:, WP:WP + C], start=False, stop=True)
                        i.then_inc(s_lin, 1)
                    if exists(t) and s == 5:
                        v_piece()
                    if exists(t + 2) and s == 6:
                        wait(pe, s_mT, done(t - 1))
                        wait(pe, s_OT, done(t - 3))
                        x_transposes(pe, t + 3)
            attention_phase(pe, step)

        @block.vector
        def _(dve):
            chain = [0]

            def link(i):
                chain[0] += 1
                i.then_inc(s_link, 1)
                dve.wait_ge(s_link, chain[0])

            for k in (*QAg, *KAg):
                nc.vector.memset(k[:, :, :, :], 0.0)
            for k in xT:
                nc.vector.memset(k[:, :, :], 0.0)
            nc.vector.memset(xtok[:, :, 2 * C:HL], SX)
            nc.vector.memset(xtok[:, :, HL:FULL], 0.0)
            nc.vector.memset(otok[:, :, 2 * C:HL], SO)
            nc.vector.memset(otok[:, :, HL:FULL], 0.0)
            nc.vector.memset(on[:, :, :], 0.0)
            nc.vector.memset(OT[:, TOK:TOK + FULL - PT], 0.0)
            for k in (*ph, *pl):
                nc.vector.memset(k[:, :, :, N:GP], 1.0)
            nc.vector.memset(m16[:, :], 0.0)
            dve.wait_ge(s_const, NCONST)
            dve.wait_ge(s_prep_p, 2)
            row = w32[2 * C:HL, :]
            link(nc.vector.tensor_tensor(row[:, 0:WF1], row[:, 0:WF1], banks[0][2 * C:HL, 0:WF1], ALU.add))
            link(nc.vector.tensor_tensor(row[:, WF1:WP], row[:, WF1:WP], banks[1][2 * C:HL, 0:WP - WF1], ALU.add))
            link(nc.vector.tensor_scalar(w32[0:2 * C, 0:WF1], w32[0:2 * C, 0:WF1], gain[:, 0:1], None, ALU.mult))
            link(nc.vector.tensor_scalar(w32[0:2 * C, WF1:WP], w32[0:2 * C, WF1:WP], gain[:, 1:2], None, ALU.mult))
            link(nc.vector.tensor_scalar(w32[:, WQ:WQ + FULL], w32[:, WQ:WQ + FULL], float(HD ** -0.5), None, ALU.mult))
            link(nc.vector.tensor_scalar(wh[:, :], w32[:, :], SWT, None, ALU.mult))
            link(nc.vector.scalar_tensor_tensor(wl[:, :], w32[:, :], SWT, wh[:, :], ALU.mult, ALU.subtract))
            link(nc.vector.tensor_scalar(w2h[:, :, :], w2f[:, :, :], SWT, None, ALU.mult))
            f = "p a n -> p (a n)"
            link(nc.vector.scalar_tensor_tensor(w2l[:, :, :].rearrange(f), w2f[:, :, :].rearrange(f), SWT,
                                                w2h[:, :, :].rearrange(f), ALU.mult, ALU.subtract))
            for k, (hi, lo) in enumerate(((bs_h, None), (bt_h, bt_l))):
                for a in range(4):
                    both = p32[a][:, 0, :, :].rearrange(f)
                    link(nc.vector.tensor_tensor(both, mask32[:, a, :], rpb32[:, k, :], ALU.add))
                    link(nc.vector.tensor_scalar(hi[:, a, :], both, SB, None, ALU.mult))
                    if lo is not None:
                        link(nc.vector.scalar_tensor_tensor(lo[:, a, :], both, SB, hi[:, a, :], ALU.mult, ALU.subtract))
            nc.vector.memset(rowmax[:, :, :], 0.0).then_inc(s_prep, 1)

            flat = "p w n -> p (w n)"

            def step(t, par, late):
                new = 1 - par

                def k_low(j):
                    dve.wait_ge(s_high, 4 * done(t) + j + 1)
                    part = KA[new][GP:FULL, 8 * j:8 * j + 8, :].rearrange(flat)
                    nc.vector.scalar_tensor_tensor(part, lin[GP:FULL, 0:HALF], SQ / (SX * SWT), part,
                                                   ALU.mult, ALU.subtract).then_inc(s_linfree, 1)

                def q_low(j):
                    dve.wait_ge(s_high, 4 * done(t) + j + 3)
                    if j == 0:
                        wait(dve, s_qbh, done(t - 1))
                    nc.vector.scalar_tensor_tensor(QB[new][:, 8 * j:8 * j + 8, :].rearrange(flat), lin[:, 0:HALF],
                                                   SQ / (SX * SWT), QA[new][:, 8 * j:8 * j + 8, :].rearrange(flat),
                                                   ALU.mult, ALU.subtract).then_inc(s_linfree, 1)

                def v_low():
                    dve.wait_ge(s_vhigh, done(t))
                    for w in range(2):
                        for g in range(G):
                            i = nc.vector.scalar_tensor_tensor(v_dst(Vl, par, w, g), v_src(w, g), SV / (SX * SWT),
                                                               v_dst(Vh, par, w, g), ALU.mult, ALU.subtract)
                    i.then_inc(s_linfree, 1)

                def blocks(dst, src, rows, k):
                    return nc.vector.tensor_scalar(dst, src[:, :, :], rows[:, k:k + 1], None, ALU.mult)

                def rmax(p):
                    dve.wait_ge(s_s, PAIRS * t + p + 1)
                    if p == 0:
                        wait(dve, s_m16, done(t - 1))
                    nc.vector.tensor_reduce(rowmax[:, 2 * p:2 * p + 2, :],
                                            sc[p % 2][0:AP_, 0:2 * COLS].rearrange("p (a n) -> p a n", n=N),
                                            AX.X, ALU.max).then_inc(s_max, 1)

                def normalize(b):
                    dve.wait_ge(s_pv, PAIRS * (t - 2) + 4 * b + 4)
                    o = po[b][0:AP_, 0:4 * HP * 2 * G * CP].rearrange("p (a d) -> p a d", d=CP)
                    nc.vector.reciprocal(rsum[:, b, :], o[:, :, HD]).then_inc(s_rsum, 1)
                    dve.wait_ge(s_rsum, 2 * (t - 2) + b + 1)
                    for w in range(2):
                        r = slice(w * GP, w * GP + N)
                        src = po[b][r, 0:4 * HP * 2 * G * CP].rearrange("p (a w g d) -> p a w g d", w=2, g=G, d=CP)[:, :, w, :, 0:HD]
                        rs = rsum[r, b, :].rearrange("p (a w g) -> p a w g", w=2, g=G)[:, :, w, :]
                        dst = on[r, 4 * b:4 * b + 4, :].rearrange("p a (h g d) -> p (a h) g d", g=G, d=HD)
                        i = nc.vector.tensor_tensor(dst, src, rs.unsqueeze(3).to_broadcast([N, 4 * HP, G, HD]), ALU.mult)
                    i.then_inc(s_norm, 1)

                for s in range(PAIRS):
                    if exists(t + 2) and s == 0:
                        dve.wait_ge(s_x[par], 8 * (t + 2 - par) + 16)
                        ln_mean(dve, t + 2, t + 3)
                    if exists(t):
                        rmax(s)
                    if exists(t + 1):
                        if s < 2:
                            k_low(s)
                        elif s < 4:
                            q_low(s - 2)
                        if s == 1:
                            dve.wait_ge(s_linfree, lin_at(t, 1) + 1)
                        if s == 1 or s == 2:
                            for hp in ((0,), (1, 2))[s - 1]:
                                blocks(KAh[new][:, hp, :, :], KA[new], headrow, hp)
                        if s == 4:
                            dve.wait_ge(s_high, 4 * done(t + 1))
                            for g in range(G):
                                i = blocks(QAg[new][:, :, g, 0:N], QA[new], grow, g)
                            i.then_inc(s_sb, 1)
                    if exists(t - 1) and s == 0:
                        dve.wait_ge(s_mtp, done(t - 1))
                        wait(dve, s_mrow, 16 * G * done(t - 2))
                        nc.vector.tensor_copy(mT[:, :], psT[0:HP * UW, 0:AP_]).then_inc(s_mT, 1)
                    if exists(t - 2) and s == 2:
                        normalize(0)
                    if exists(t + 2) and s == 3:
                        ln_variance(dve, t + 3)
                    if exists(t - 3) and s == 5:
                        dve.wait_ge(s_lin, lin_at(t, 4) + 1)
                        y = lin[0:PT, 0:CH * C].rearrange("p (c n) -> p c n", n=C)
                        nc.vector.scalar_tensor_tensor(x_of(t - 3), y, 1.0 / (SO * SWT), x_of(t - 3),
                                                       ALU.mult, ALU.add).then_inc(s_linfree, 1)
                    if exists(t):
                        if s == 4:
                            wait(dve, s_st, PAIRS * done(t - 2))
                            blocks(KAg[par][:, :, 0, 0:N], KA[par], grow, 0)
                        if s == 5:
                            blocks(KAg[par][:, :, 1, 0:N], KA[par], grow, 1)
                            blocks(QAh[par][:, 0, :, :], QA[par], headrow, 0)
                        if s == 7:
                            blocks(QAh[par][:, 1, :, :], QA[par], headrow, 1)
                            blocks(QAh[par][:, 2, :, :], QA[par], headrow, 2).then_inc(s_tb, 1)
                    if exists(t - 2) and s == 5:
                        normalize(1)
                    if exists(t) and s == 7:
                        v_low()
                    if exists(t + 2) and s == 6:
                        ln_low(dve, t + 3)
                    if exists(t - 2) and s == 7:
                        dve.wait_ge(s_ohi, done(t - 2))
                        nc.vector.tensor_tensor(otok[:, :, C:2 * C], on[:, :, :], otok[:, :, 0:C],
                                                ALU.subtract).then_inc(s_olo, 1)
                    if exists(t) and s == 7:
                        dve.wait_ge(s_max, PAIRS * done(t))
                        nc.vector.tensor_scalar(m16[:, 0:HP * UW].rearrange("p (a w) -> p a w", a=HP),
                                                rowmax[:, :, :].rearrange("p w a -> p a w"), -1.0 / SM, LOGP * SB / SM,
                                                ALU.mult, ALU.add).then_inc(s_m16, 1)
            attention_phase(dve, step)

        actx.close()

        hT = sb("hT", [HL, TOK], f16)
        gel = sb("gel", [128, 3, HTOK], f32)
        gh = [sb(f"gh{i}", [128, 3, GW], f16) for i in range(2)]
        gl = [sb(f"gl{i}", [128, 3, GW], f16) for i in range(2)]
        ybuf = [sb(f"ybuf{i}", [PT, CH * C], f32) for i in range(2)]

        def mlp_phase(e, step):
            for t in range(-2, 4):
                step(t, t % 2)
            with e.Fori(4, UNITS - 3, 2) as i:
                step(i, 0)
                step(i + 1, 1)
            for t in range(UNITS - 2, UNITS + 1):
                step(t, t % 2)

        block = ctx.enter_context(nc.Block())

        @block.sync
        def _(sp):
            def step(t, par):
                if exists(t - 1):
                    sp.wait_ge(s_yo, done(t - 1))
                    sp.dma_start(out[bass.ds(t - 1, 1), :, :].rearrange("u p n -> p (u n)"),
                                 ybuf[1 - par][:, :]).then_inc(s_store[1 - par], 16)
            mlp_phase(sp, step)
            for par in range(2):
                sp.wait_ge(s_store[par], 16 * UNITS // 2)

        @block.gpsimd
        def _(pool):
            def step(t, par):
                if exists(t + 2):
                    n = t + 3 + UNITS
                    ln_centre(pool, t + 2, n)
                    nc.gpsimd.tensor_tensor(x_of(t + 2), x_of(t + 2), b2t[:, :].unsqueeze(1).to_broadcast([PT, CH, C]),
                                            ALU.add).then_inc(s_x1b, 1)
                    ln_rsqrt(pool, n)
                    ln_scale(pool, n)
            mlp_phase(pool, step)

        @block.scalar
        def _(act):
            def step(t, par):
                def gelu(k):
                    act.wait_ge(s_h, 3 * t + k + 1)
                    wait(act, s_gl, 3 * (t - 1) + k + 1)
                    hb = banks[3 * par + k]
                    cols = HTOK if k == 0 else 3 * PT
                    i = nc.scalar.activation(gel[:, k, 0:cols], hb[:, 0:cols], ACT.Gelu, scale=1.0 / (SX * SWT))
                    if k == 2:
                        i = nc.scalar.activation(gel[0:64, k, cols:HTOK], hb[0:64, cols:HTOK], ACT.Gelu,
                                                 scale=1.0 / (SX * SWT))
                    i.then_inc(s_g, 1)

                n = t + 3 + UNITS
                if exists(t):
                    if isinstance(t, int) and t == 0:
                        act.wait_ge(s_pads, 1)
                    gelu(0)
                if exists(t + 2):
                    ln_square(act, n)
                if exists(t + 1):
                    act.wait_ge(s_xtp, n - 1)
                    nc.scalar.activation(hT[:, :], psT[0:HL, 0:TOK], ACT.Copy).then_inc(s_xT, 1)
                if exists(t):
                    gelu(1)
                    gelu(2)
                if exists(t + 2):
                    ln_high(act, n)
            mlp_phase(act, step)

        @block.tensor
        def _(pe):
            def step(t, par):
                if exists(t):
                    pe.wait_ge(s_xT, t + 1 + UNITS)
                    wait(pe, s_g, 3 * (t - 1))
                    for k in range(2):
                        lo, hi = (0, HTOK) if k == 0 else (HTOK, TOK)
                        dst = banks[3 * par + k][:, 0:hi - lo]
                        nc.tensor.matmul(dst, wh[:, WF1:WF1 + FULL], hT[:, lo:hi], start=True, stop=False)
                        nc.tensor.matmul(dst, wl[:, WF1:WF1 + FULL], hT[:, lo:hi], start=False, stop=True).then_inc(s_h, 1)
                    for k in range(2):
                        lo, hi = (0, HTOK) if k == 0 else (HTOK, TOK)
                        col = WF1B + k * FULL
                        for m, wt in enumerate((wh, wl)):
                            i = nc.tensor.matmul(banks[3 * par + 2][:, 0:hi - lo], wt[:, col:col + FULL], hT[:, lo:hi],
                                                 start=(k == 0 and m == 0), stop=(k == 1 and m == 1), skip_group_check=True)
                    i.then_inc(s_h, 1)
                if exists(t + 1):
                    pe.wait_ge(s_xT, t + 1 + UNITS)
                    x_transposes(pe, t + 2 + UNITS)
                if exists(t - 1):
                    pe.wait_ge(s_gl, 3 * t)
                    wait(pe, s_yo, t - 1)
                    for c in range(CH):
                        k, at = c // 4, (c % 4) * PT
                        dst = banks[6][:, c * C:(c + 1) * C]
                        terms = [(a[1 - par], r, wt, j) for r, j in ((k, 0), (2, 1 + k))
                                 for a, wt in ((gh, w2h), (gh, w2l), (gl, w2h))]
                        for m, (a, r, wt, j) in enumerate(terms):
                            i = nc.tensor.matmul(dst, a[:, r, at:at + FULL], wt[:, j, :], start=(m == 0), stop=(m == 5))
                    i.then_inc(s_y, 1)
            mlp_phase(pe, step)

        @block.vector
        def _(dve):
            nc.vector.memset(gel[64:128, 2, 3 * PT:HTOK], 0.0)
            for k in (*gh, *gl):
                i = nc.vector.memset(k[:, :, :], 0.0)
            i.then_inc(s_pads, 1)

            def step(t, par):
                def split(k):
                    dve.wait_ge(s_g, 3 * t + k + 1)
                    if k == 0:
                        wait(dve, s_y, t - 1)
                    cols = 3 * PT if k == 1 else HTOK
                    nc.vector.tensor_scalar(gh[par][:, k, 0:cols], gel[:, k, 0:cols], SG, None, ALU.mult).then_inc(s_gs, 1)
                    dve.wait_ge(s_gs, 3 * t + k + 1)
                    nc.vector.scalar_tensor_tensor(gl[par][:, k, 0:cols], gel[:, k, 0:cols], SG, gh[par][:, k, 0:cols],
                                                   ALU.mult, ALU.subtract).then_inc(s_gl, 1)

                n = t + 3 + UNITS
                if exists(t + 1):
                    ln_low(dve, n - 1)
                if exists(t + 2):
                    ln_mean(dve, t + 2, n)
                if exists(t):
                    split(0)
                if exists(t + 2):
                    ln_variance(dve, n)
                if exists(t):
                    split(1)
                    split(2)
                if exists(t - 1):
                    dve.wait_ge(s_y, done(t - 1))
                    dve.wait_ge(s_x1b, done(t - 1))
                    wait(dve, s_store[1 - par], 8 * (t - 1 - (1 - par)))
                    nc.vector.scalar_tensor_tensor(ybuf[1 - par][:, :].rearrange("p (c n) -> p c n", n=C),
                                                   banks[6][0:PT, 0:CH * C].rearrange("p (c n) -> p c n", n=C),
                                                   1.0 / (SG * SWT), x_of(t - 1), ALU.mult, ALU.add).then_inc(s_yo, 1)
            mlp_phase(dve, step)


def _windows(x):
    x = np.roll(x, (-SS, -SS), axis=(1, 2)).reshape(B, H // WS, WS, NWX, WS, C)
    x = x.transpose(1, 0, 3, 2, 4, 5).reshape(UNITS, CH, PT, C)
    return np.ascontiguousarray(x.transpose(0, 2, 1, 3)).reshape(UNITS, PT, CH * C)


def _image(y):
    y = y.reshape(UNITS, PT, CH, C).transpose(0, 2, 1, 3).reshape(H // WS, B, NWX, WS, WS, C)
    y = y.transpose(1, 0, 3, 2, 4, 5).reshape(B, H, W, C)
    return np.ascontiguousarray(np.roll(y, (SS, SS), axis=(1, 2)))


def _weights(qkv_w, qkv_b, proj_w, proj_b, fc1_w, fc1_b):
    def stack(w, b):
        return np.concatenate([w, w, b[None]], axis=0)

    qkv = stack(qkv_w, qkv_b)
    w = np.zeros((HL, WCOLS), np.float32)
    for k, at in enumerate((WQ, WK)):
        cols = qkv[:, k * C:(k + 1) * C].reshape(HL, HP, G, HD)
        for quadrant in range(4):
            c = at + quadrant * KQ
            w[:, c:c + KD] = cols[:, :, quadrant % 2, :].reshape(HL, KD)
    w[2 * C, WK + MROW:WK + MROW + G] = SM / SQ
    w[:, WV:WV + C] = qkv[:, 2 * C:3 * C]
    fc1 = stack(fc1_w, fc1_b)
    w[:, WF1:WF1 + 128] = fc1[:, 0:128]
    w[:, WF1B:WF1B + 64] = fc1[:, 128:HID]
    w[:, WF1B + FULL + 64:WF1B + 2 * FULL] = fc1[:, 128:HID]
    w[:, WP:WP + C] = stack(proj_w, proj_b)
    return w


def _position_bias(table):
    i = np.arange(N)
    r, c = i // WS, i % WS
    at = (r[:, None] - r[None, :] + WS - 1) * (2 * WS - 1) + (c[:, None] - c[None, :] + WS - 1)
    out = np.zeros((AP_, 2, HP, N), np.float32)
    for g in range(G):
        for hp in range(HP):
            m = table[:, 2 * hp + g][at]
            out[g * GP:g * GP + N, 0, hp] = m
            out[g * GP:g * GP + N, 1, hp] = m.T
    return out.reshape(AP_, 2, COLS)


def _window_mask():
    out = np.zeros((AP_, 4, HP, N), np.float32)
    i = np.arange(N)
    for kind in range(4):
        row = (i // WS >= WS - SS) if kind // 2 else np.zeros(N, bool)
        col = (i % WS >= WS - SS) if kind % 2 else np.zeros(N, bool)
        region = 2 * row + col
        m = np.where(region[:, None] != region[None, :], -100.0, 0.0)
        for g in range(G):
            out[g * GP:g * GP + N, kind] = m[:, None, :]
    return out.reshape(AP_, 4, COLS)


def kernel(**inputs):
    import concourse.bacc as bacc
    from concourse.bass_utils import run_bass_kernel_spmd

    p = {k.replace("L0_conv_", ""): np.asarray(v) for k, v in inputs.items()}
    shifts = np.zeros((C, 2, HL), np.float32)
    shifts[:, 0, 2 * C] = p["norm1_b"]
    shifts[:, 1, 2 * C] = p["norm2_b"]
    gains = np.stack([np.concatenate([p[k]] * 2) for k in ("norm1_g", "norm2_g")], axis=1)
    headrow = np.zeros((FULL, HP), np.float32)
    grow = np.zeros((FULL, G), np.float32)
    for quadrant in range(4):
        for hp in range(HP):
            headrow[quadrant * KQ + hp * HD:quadrant * KQ + (hp + 1) * HD, hp] = 1.0
        grow[quadrant * KQ:quadrant * KQ + KD, quadrant % 2] = 1.0
    for g in range(G):
        grow[MROW + g, g] = 1.0
    w2 = np.zeros((128, 3, C), np.float32)
    w2[:, 0] = p["fc2_w"][0:128]
    for k in range(2):
        w2[64 * k:64 * k + 64, 1 + k] = p["fc2_w"][128:HID]
    onescol = np.zeros((2, AP_, 2, PAIRS, HP, G, CP), np.float16)
    for g in range(G):
        onescol[0, g * GP:g * GP + N, :, :, :, g, HD] = SV / SO
    arrays = {
        "x": _windows(p["x"]),
        "weights": _weights(p["qkv_w"], p["qkv_b"], p["proj_w"], p["proj_b"], p["fc1_w"], p["fc1_b"]),
        "gains": gains,
        "shifts": shifts,
        "w2": w2,
        "b2": np.ascontiguousarray(np.broadcast_to(p["fc2_b"], (PT, C))),
        "rpb": _position_bias(p["rpb_table"]),
        "headrow": headrow,
        "grow": grow,
        "maskt": _window_mask(),
        "ident": np.eye(128, dtype=np.float16),
        "onescol": onescol.reshape(2, AP_, 2, PAIRS, HP, G * CP),
    }
    nc = bacc.Bacc("TRN2", target_bir_lowering=False, num_devices=1)
    args = [nc.dram_tensor(f"in_{k}", a.shape, mybir.dt.from_np(a.dtype), kind="ExternalInput").ap()
            for k, a in arrays.items()]
    out = nc.dram_tensor("out_y", (UNITS, PT, CH * C), mybir.dt.float32, kind="ExternalOutput").ap()
    swin_block_kernel(nc, *args, out)
    r = run_bass_kernel_spmd(nc, [{f"in_{k}": a for k, a in arrays.items()}], core_ids=[0])
    return _image(r.results[0]["out_y"])
```

```python
import numpy as np
import concourse.bass as bass
from concourse import mybir
from contextlib import ExitStack

B, H, W, C = 16, 56, 56, 48
WS, SS, NH = 7, 3, 6
N = WS * WS
HD = C // NH
HID = 4 * C
NWX = W // WS
EPS = 1e-5

UW = 16
UNITS = B * (H // WS) * NWX // UW
EDGE = UNITS - UNITS // (H // WS)
TOK = UW * N
CH = 7
PT = TOK // CH
HALF = TOK // 2
PAIRS = UW // 2
G, HP = 2, 3
GP = 64
AP_ = GP + N
FULL = 128
KQ = 32
KD = HP * HD
MROW = KQ + KD
HL = 2 * C + 1
COLS = HP * N
CP = HD + 1

SX, SWT = 4096.0, 64.0
SQ = 16.0
SB = SQ * SQ
SM = 4096.0
SV = 64.0
SO = 256.0
LOGP = 8 * float(np.log(2.0))

WQ = 0
WK = FULL
WV = 2 * FULL
WF1 = WV + C
WF1B = WF1 + FULL
WP = WF1B + 2 * FULL
WCOLS = WP + C
HTOK = 4 * PT
GW = HTOK + FULL - PT

TLAG = 3
PLAG = 5


def exists(u):
    return not isinstance(u, int) or 0 <= u < UNITS


def done(u):
    return min(max(u + 1, 0), UNITS) if isinstance(u, int) else u + 1


def wait(engine, semaphore, value):
    if not (isinstance(value, int) and value <= 0):
        engine.wait_ge(semaphore, value)


def t_pair(t, slot):
    return (t - 1, slot - TLAG) if slot >= TLAG else (t - 2, slot - TLAG + PAIRS)


def v_pair(t, slot):
    return (t - 1, slot - PLAG) if slot >= PLAG else (t - 2, slot - PLAG + PAIRS)


def lin_at(t, k):
    if not isinstance(t, int):
        return 6 * t + 1 + k
    return (4 * done(t) + (min(k, 4) if exists(t + 1) else 0) + done(t - 4) + (1 if k > 4 and exists(t - 3) else 0)
            + done(t - 1) + (1 if k > 5 and exists(t) else 0))


def swin_block_kernel(nc, x, weights, gains, shifts, w2, b2, rpb, headrow_d, grow_d, maskt, ident, onescol, out):
    f32, f16 = mybir.dt.float32, mybir.dt.float16
    ALU, ACT, AX = mybir.AluOpType, mybir.ActivationFunctionType, mybir.AxisListType
    ctx = ExitStack()
    with ctx:
        def sb(name, shape, dt, within=ctx):
            return within.enter_context(nc.sbuf_tensor(name, shape, dt))

        def sem(name):
            return ctx.enter_context(nc.semaphore(name))

        xres = sb("xres", [PT, UNITS, CH * C], f32)
        nmean = sb("nmean", [PT, CH], f32)
        xc = [sb(f"xc{i}", [PT, CH, C], f32) for i in range(2)]
        sq = sb("sq", [PT, CH, C], f32)
        ssum = sb("ssum", [PT, CH], f32)
        sqsum = sb("sqsum", [PT, CH], f32)
        var = sb("var", [PT, CH], f32)
        rstd = sb("rstd", [PT, CH], f32)
        mhalf = sb("mhalf", [PT, CH], f32)
        xn = sb("xn", [PT, CH, C], f32)
        xtok = sb("xtok", [PT, CH, FULL], f16)
        wh = sb("wh", [HL, WCOLS], f16)
        wl = sb("wl", [HL, WCOLS], f16)
        w2h = sb("w2h", [128, 3, C], f16)
        w2l = sb("w2l", [128, 3, C], f16)
        b2t = sb("b2t", [PT, C], f32)
        idt = sb("idt", [FULL, FULL], f16)

        banks = [ctx.enter_context(nc.psum_tensor(f"bank{i}", [128, 512], f32)) for i in range(7)]
        psT = ctx.enter_context(nc.psum_tensor("psT", [128, 1024], f16))
        lin, sc, st, po = banks[0], banks[1:3], banks[3:5], banks[5:7]

        s_x = [sem(f"x_loaded{i}") for i in range(2)]
        s_const = sem("constants_loaded")
        s_prep = sem("weights_prepared")
        s_prep_p = sem("shift_products")
        s_link = sem("preparation_chain")
        s_sum = sem("sums_ready")
        s_sqsum = sem("sums_of_squares_ready")
        s_mean = sem("mean_ready")
        s_xc = sem("centred")
        s_sq = sem("squared")
        s_var = sem("variance_ready")
        s_pow = sem("rstd_ready")
        s_xn = sem("normalized")
        s_xhi = sem("x_high_ready")
        s_xlo = sem("x_low_ready")
        s_xtp = sem("x_transposed")
        s_xT = sem("xT_ready")
        s_lin = sem("lin_full")
        s_linfree = sem("lin_free")
        s_high = sem("qk_high_ready")
        s_vhigh = sem("v_high_ready")
        s_sb = sem("score_operands_ready")
        s_tb = sem("tscore_operands_ready")
        s_qbh = sem("q_low_blocks_ready")
        s_s = sem("scores_full")
        s_max = sem("rowmax_ready")
        s_m16 = sem("m16_ready")
        s_mtp = sem("m_transposed")
        s_mT = sem("mT_ready")
        s_mrow = sem("m_rows_written")
        s_st = sem("tscores_full")
        s_exp = sem("probs_ready")
        s_pl = sem("probs_low_ready")
        s_pv = sem("pv_done")
        s_rsum = sem("rsum_ready")
        s_norm = sem("attention_normalized")
        s_ohi = sem("o_high_ready")
        s_olo = sem("o_low_ready")
        s_otp = sem("o_transposed")
        s_OT = sem("OT_ready")
        s_pads = sem("mlp_pads_ready")
        s_h = sem("hidden_full")
        s_g = sem("gelu_ready")
        s_gl = sem("gelu_low_ready")
        s_x1b = sem("x1_with_bias")
        s_y = sem("y_full")
        s_yo = sem("y_ready")
        s_store = [sem(f"stored{i}") for i in range(2)]

        NCONST = 16 * 14

        def x_of(u):
            return xres[:, bass.ds(u, 1), :].rearrange("p u (c n) -> p (u c) n", n=C)

        def ln_sum(dve, u):
            nc.vector.tensor_reduce(ssum[:, :], x_of(u), AX.X, ALU.add).then_inc(s_sum, 1)

        def ln_mean(dve, n):
            dve.wait_ge(s_sum, n)
            nc.vector.tensor_scalar(nmean[:, :], ssum[:, :], -1.0 / C, None, ALU.mult).then_inc(s_mean, 1)

        def ln_centre(pool, u, par, n):
            wait(pool, s_xn, n - 2)
            pool.wait_ge(s_mean, n)
            nc.gpsimd.tensor_tensor(xc[par][:, :, :], x_of(u), nmean[:, :].unsqueeze(2).to_broadcast([PT, CH, C]),
                                    ALU.add).then_inc(s_xc, 1)

        def ln_square(act, par, n):
            wait(act, s_sqsum, n - 1)
            act.wait_ge(s_xc, n)
            nc.scalar.activation(sq[:, :, :], xc[par][:, :, :], ACT.Square).then_inc(s_sq, 1)

        def ln_sum_squares(dve, n):
            dve.wait_ge(s_sq, n)
            wait(dve, s_var, n - 1)
            nc.vector.tensor_reduce(sqsum[:, :], sq[:, :, :], AX.X, ALU.add).then_inc(s_sqsum, 1)

        def ln_variance(dve, n):
            dve.wait_ge(s_sqsum, n)
            nc.vector.tensor_scalar(var[:, :], sqsum[:, :], 1.0 / C, EPS, ALU.mult, ALU.add).then_inc(s_var, 1)

        def ln_rsqrt(pool, n):
            wait(pool, s_xn, n - 1)
            pool.wait_ge(s_var, n)
            nc.gpsimd.tensor_tensor(rstd[:, :], var[:, :], mhalf[:, :], ALU.pow).then_inc(s_pow, 1)

        def ln_scale(pool, par, n):
            wait(pool, s_xlo, n - 1)
            pool.wait_ge(s_pow, n + 1)
            nc.gpsimd.tensor_tensor(xn[:, :, :], xc[par][:, :, :], rstd[:, :].unsqueeze(2).to_broadcast([PT, CH, C]),
                                    ALU.mult).then_inc(s_xn, 1)

        def ln_high(act, n):
            act.wait_ge(s_xn, n)
            wait(act, s_xtp, n - 1)
            nc.scalar.activation(xtok[:, :, 0:C], xn[:, :, :], ACT.Copy, scale=SX).then_inc(s_xhi, 1)

        def ln_low(dve, n):
            dve.wait_ge(s_xhi, n)
            nc.vector.scalar_tensor_tensor(xtok[:, :, C:2 * C], xn[:, :, :], SX, xtok[:, :, 0:C],
                                           ALU.mult, ALU.subtract).then_inc(s_xlo, 1)

        def x_transposes(pe, n):
            pe.wait_ge(s_xlo, n)
            for c in range(CH):
                i = nc.tensor.transpose(psT[:, c * PT:(c + 1) * PT], xtok[:, c, :], idt[0:PT, 0:PT])
            i.then_inc(s_xtp, 1)

        actx = ExitStack()
        ctx.enter_context(actx)

        def sba(name, shape, dt):
            return sb(name, shape, dt, actx)

        w32 = sba("w32", [HL, WCOLS], f32)
        gain = sba("gain", [2 * C, 2], f32)
        shift = sba("shift", [C, 2, HL], f32)
        w2f = sba("w2f", [128, 3, C], f32)
        rpb32 = sba("rpb32", [AP_, 2, COLS], f32)
        mask32 = sba("mask32", [AP_, 4, COLS], f32)
        bs_h = sba("bs_h", [AP_, 4, COLS], f16)
        bt_h = sba("bt_h", [AP_, 4, COLS], f16)
        bt_l = sba("bt_l", [AP_, 4, COLS], f16)
        headrow = sba("headrow", [FULL, HP], f32)
        grow = sba("grow", [FULL, G], f32)
        xT = [sba(f"xT{i}", [HL, UW, GP], f16) for i in range(2)]
        QA = [sba(f"QA{i}", [FULL, UW, N], f16) for i in range(2)]
        KA = [sba(f"KA{i}", [FULL, UW, N], f16) for i in range(2)]
        QB = [sba(f"QB{i}", [FULL, UW, N], f16) for i in range(2)]
        QAg = [sba(f"QAg{i}", [FULL, UW, G, GP], f16) for i in range(2)]
        KAh = [sba(f"KAh{i}", [FULL, HP, UW, N], f16) for i in range(2)]
        KAg = [sba(f"KAg{i}", [FULL, UW, G, GP], f16) for i in range(2)]
        QAh = [sba(f"QAh{i}", [FULL, HP, UW, N], f16) for i in range(2)]
        QBh = [sba(f"QBh{i}", [FULL, HP, UW, N], f16) for i in range(2)]
        Vh = [sba(f"Vh{i}", [AP_, 2, PAIRS, HP, G * CP], f16) for i in range(2)]
        Vl = [sba(f"Vl{i}", [AP_, 2, PAIRS, HP, G * CP], f16) for i in range(2)]
        rowmax = sba("rowmax", [AP_, UW, HP], f32)
        m16 = sba("m16", [AP_, FULL], f16)
        mT = sba("mT", [HP * UW, AP_], f16)
        p32 = [sba(f"p32_{i}", [AP_, 2, HP, N], f32) for i in range(4)]
        ph = [sba(f"ph{i}", [AP_, HP, 2, GP], f16) for i in range(4)]
        pl = [sba(f"pl{i}", [AP_, HP, 2, GP], f16) for i in range(4)]
        rsum = sba("rsum", [AP_, 2, 4 * HP * 2 * G], f32)
        on = sba("on", [AP_, PAIRS, C], f32)
        otok = sba("otok", [AP_, PAIRS, FULL], f16)
        OT = sba("OT", [HL, TOK + FULL - PT], f16)

        def v_src(w, g):
            return lin[w * GP:w * GP + N, 0:PAIRS * C].rearrange("p (a g d) -> p a g d", g=G, d=HD)[:, :, g, :]

        def v_dst(V, par, w, g):
            return V[par][g * GP:g * GP + N, w, :, :, g * CP:g * CP + HD].rearrange("p a h d -> p (a h) d")

        def attention_phase(e, step, prepare):
            step(-2, 0, False)
            if prepare:
                prepare()
            for t in range(-1, 3):
                step(t, t % 2, False)
            with e.Fori(3, EDGE - 2, 2) as i:
                step(i, 1, False)
                step(i + 1, 0, False)
            for t in range(EDGE - 1, EDGE + 2):
                step(t, t % 2, False)
            with e.Fori(EDGE + 2, UNITS - 3, 2) as i:
                step(i, 0, True)
                step(i + 1, 1, True)
            for t in range(UNITS - 2, UNITS + 3):
                step(t, t % 2, True)

        def wrapped(u, late):
            return u >= EDGE if isinstance(u, int) else late

        block = actx.enter_context(nc.Block())

        @block.sync
        def _(sp):
            def load(u, par):
                wait(sp, s_x[par], 8 * (u - par))
                sp.dma_start(xres[:, bass.ds(u, 1), :], x[bass.ds(u, 1), :, :].rearrange("u p n -> p u n")).then_inc(s_x[par], 16)
            for u in range(2):
                load(u, u % 2)
            for dst, src in ((w32, weights), (gain, gains), (shift, shifts), (w2f, w2), (b2t, b2), (rpb32, rpb),
                             (mask32, maskt), (idt, ident), (headrow, headrow_d), (grow, grow_d), (Vh[0], onescol[0]),
                             (Vh[1], onescol[0]), (Vl[0], onescol[1]), (Vl[1], onescol[1])):
                sp.dma_start(dst[:], src).then_inc(s_const, 16)
            load(2, 0)

            def step(t, par, late):
                if exists(t + 5) and not late:
                    load(t + 5, 1 - par)
                if isinstance(t, int) and t == EDGE + 1:
                    load(t + 6, par)
                if exists(t - 1):
                    sp.wait_ge(s_mT, done(t - 1))
                    sp.wait_ge(s_qbh, done(t - 1))
                    for g in range(G):
                        sp.dma_start(QBh[1 - par][MROW + g:MROW + g + 1, :, :, :].rearrange("o a w n -> o (a w) n"),
                                     mT[:, g * GP:g * GP + N]).then_inc(s_mrow, 16)
            attention_phase(sp, step, None)

        @block.gpsimd
        def _(pool):
            nc.gpsimd.memset(mhalf[:, :], -0.5).then_inc(s_pow, 1)
            pool.wait_ge(s_pow, 1)

            def step(t, par, late):
                def low(u, p):
                    pool.wait_ge(s_exp, PAIRS * u + p + 1)
                    nc.gpsimd.tensor_tensor(pl[p % 4][:, :, :, 0:N].rearrange("p a w n -> p w a n"), p32[p % 4][:, :, :, :],
                                            ph[p % 4][:, :, :, 0:N].rearrange("p a w n -> p w a n"),
                                            ALU.subtract).then_inc(s_pl, 1)

                for s in range(PAIRS):
                    u, p = t_pair(t, s)
                    if exists(u):
                        low(u, p)
                    if exists(t + 2):
                        if s == 1:
                            ln_centre(pool, t + 2, par, t + 3)
                        if s == 3:
                            ln_rsqrt(pool, t + 3)
                        if s == 4:
                            ln_scale(pool, par, t + 3)
                    if exists(t) and s >= 5:
                        hp = s - 5
                        dst, src = QBh[par][:, hp, :, :], QB[par]
                        lo = 0
                        if hp == 0:
                            pool.wait_ge(s_linfree, lin_at(t, 0))
                            nc.gpsimd.tensor_tensor(dst[:, 0, :], src[:, 0, :], headrow[:, 0:1].to_broadcast([FULL, N]),
                                                    ALU.mult)
                            lo = 1
                        i = nc.gpsimd.tensor_scalar(dst[:, lo:UW, :].rearrange("p w n -> p (w n)"),
                                                    src[:, lo:UW, :].rearrange("p w n -> p (w n)"),
                                                    headrow[:, hp:hp + 1], 1.0, ALU.mult, ALU.mult)
                        if hp == HP - 1:
                            i.then_inc(s_qbh, 1)

            def prepare():
                pool.wait_ge(s_prep, 1)
            attention_phase(pool, step, prepare)

        @block.scalar
        def _(act):
            def step(t, par, late):
                def qk_high(j):
                    dst = (KA, QA)[j // 2][1 - par][:, 8 * (j % 2):8 * (j % 2) + 8, :].rearrange("p w n -> p (w n)")
                    act.wait_ge(s_lin, lin_at(t, j) + 1)
                    if j == 0:
                        wait(act, s_tb, 4 * done(t - 1))
                    nc.scalar.activation(dst, lin[:, 0:HALF], ACT.Copy, scale=SQ / (SX * SWT)).then_inc(s_high, 1)

                def v_high():
                    act.wait_ge(s_lin, lin_at(t, 5) + 1)
                    wait(act, s_pv, PAIRS * done(t - 2))
                    for w in range(2):
                        for g in range(G):
                            i = nc.scalar.activation(v_dst(Vh, par, w, g), v_src(w, g), ACT.Copy, scale=SV / (SX * SWT))
                    i.then_inc(s_vhigh, 1)

                def exp(u, p):
                    act.wait_ge(s_st, PAIRS * u + p + 1)
                    wait(act, s_pv, PAIRS * u + p - 3)
                    src = st[p % 2][0:AP_, 0:2 * COLS].rearrange("p (w a n) -> p w a n", w=2, n=N)
                    nc.scalar.activation(ph[p % 4][:, :, :, 0:N].rearrange("p a w n -> p w a n"), src, ACT.Exp,
                                         scale=1.0 / SB)
                    nc.scalar.activation(p32[p % 4][:, :, :, :], src, ACT.Exp, scale=1.0 / SB).then_inc(s_exp, 1)

                for s in range(PAIRS):
                    if exists(t + 1) and 1 <= s < 5:
                        qk_high(s - 1)
                    if exists(t + 2) and s == 6:
                        ln_high(act, t + 3)
                    if exists(t) and s == 6:
                        v_high()
                    u, p = t_pair(t, s)
                    if exists(u):
                        exp(u, p)
                    if exists(t - 3) and s == 1:
                        act.wait_ge(s_otp, done(t - 3))
                        nc.scalar.activation(OT[:, 0:TOK].rearrange("p (w n) -> p w n", n=N),
                                             psT[0:HL, :].rearrange("p (w n) -> p w n", n=GP)[:, :, 0:N],
                                             ACT.Copy).then_inc(s_OT, 1)
                    if exists(t + 2) and s == 2:
                        ln_square(act, par, t + 3)
                    if exists(t) and s in (3, 4):
                        if s == 3:
                            wait(act, s_st, PAIRS * done(t - 2))
                        nc.scalar.activation(QAh[par][:, s - 2, :, :], QA[par][:, :, :], ACT.Copy,
                                             scale=headrow[:, s - 2:s - 1]).then_inc(s_tb, 1)
                    if exists(t - 2) and s == 6:
                        act.wait_ge(s_norm, 2 * done(t - 2))
                        nc.scalar.activation(otok[:, :, 0:C], on[:, :, :], ACT.Copy).then_inc(s_ohi, 1)
                    if exists(t + 2) and s == 7:
                        act.wait_ge(s_xtp, done(t + 2))
                        nc.scalar.activation(xT[par][:, :, 0:N], psT[0:HL, 0:TOK].rearrange("p (w n) -> p w n", n=N),
                                             ACT.Copy).then_inc(s_xT, 1)

            def prepare():
                act.wait_ge(s_prep, 1)
            attention_phase(act, step, prepare)

        @block.tensor
        def _(pe):
            pe.wait_ge(s_const, NCONST)
            nc.tensor.matmul(banks[0][0:HL, 0:WF1], shift[:, 0, :], w32[0:C, 0:WF1], start=True, stop=True).then_inc(s_prep_p, 1)
            nc.tensor.matmul(banks[1][0:HL, 0:WP - WF1], shift[:, 1, :], w32[0:C, WF1:WP], start=True, stop=True)\
              .then_inc(s_prep_p, 1)

            def step(t, par, late):
                def lin_free(k):
                    wait(pe, s_linfree, lin_at(t, k))

                def qk_piece(j):
                    col = (WK, WQ)[j // 2]
                    if j == 0:
                        pe.wait_ge(s_xT, done(t + 1))
                    lin_free(j)
                    tok = xT[1 - par][:, 8 * (j % 2):8 * (j % 2) + 8, 0:N]
                    nc.tensor.matmul(lin[:, 0:HALF], wh[:, col:col + FULL], tok, start=True, stop=False)
                    nc.tensor.matmul(lin[:, 0:HALF], wl[:, col:col + FULL], tok, start=False, stop=True).then_inc(s_lin, 1)

                def v_piece():
                    lin_free(5)
                    for p in range(PAIRS):
                        tok = xT[par][:, 2 * p:2 * p + 2, :].rearrange("p w n -> p (w n)")
                        dst = lin[:, p * C:(p + 1) * C]
                        nc.tensor.matmul(dst, tok, wh[:, WV:WV + C], start=True, stop=False)
                        i = nc.tensor.matmul(dst, tok, wl[:, WV:WV + C], start=False, stop=True)
                    i.then_inc(s_lin, 1)

                def bias_pair(bank, table, in_last_strip, p, start):
                    kind = 2 * in_last_strip
                    if p % 4 == 3:
                        src = table[:, kind:kind + 2, :]
                    else:
                        src = table[:, kind:kind + 1, :].to_broadcast([AP_, 2, COLS])
                    nc.tensor.matmul(bank[:, 0:2 * COLS].rearrange("p (w n) -> p w n", w=2), idt[0:AP_, :], src,
                                     start=start, stop=False, skip_group_check=True)

                def scores(u, upar, p):
                    bank = sc[p % 2]
                    if p == 0:
                        pe.wait_ge(s_sb, done(u))
                    wait(pe, s_max, PAIRS * u + p - 1)
                    bias_pair(bank, bs_h, wrapped(u, late), p, True)
                    for w in range(2):
                        i = nc.tensor.matmul(bank[:, w * COLS:(w + 1) * COLS],
                                             QAg[upar][:, 2 * p + w, :, :].rearrange("p g n -> p (g n)"),
                                             KAh[upar][:, :, 2 * p + w, :], start=False, stop=True, skip_group_check=True)
                    i.then_inc(s_s, 1)

                def t_scores(u, upar, p):
                    bank = st[p % 2]
                    if p == 0:
                        pe.wait_ge(s_tb, 4 * done(u))
                        pe.wait_ge(s_mrow, 16 * G * done(u))
                    wait(pe, s_exp, PAIRS * u + p - 1)
                    bias_pair(bank, bt_h, wrapped(u, late), p, True)
                    bias_pair(bank, bt_l, wrapped(u, late), p, False)
                    for w in range(2):
                        for q in (QAh, QBh):
                            i = nc.tensor.matmul(bank[:, w * COLS:(w + 1) * COLS],
                                                 KAg[upar][:, 2 * p + w, :, :].rearrange("p g n -> p (g n)"),
                                                 q[upar][:, :, 2 * p + w, :], start=False, stop=True, skip_group_check=True)
                    i.then_inc(s_st, 1)

                def pv(u, upar, p):
                    pe.wait_ge(s_pl, PAIRS * u + p + 1)
                    if p == 0:
                        pe.wait_ge(s_linfree, lin_at(t, 0))
                    if p % 4 == 0:
                        wait(pe, s_norm, 2 * (u - 1) + p // 4 + 1)
                    for hp in range(HP):
                        at = (p % 4 * HP + hp) * 2 * G * CP
                        dst = po[p // 4][:, at:at + 2 * G * CP].rearrange("p (w n) -> p w n", w=2)
                        for k, (pr, v) in enumerate(((ph, Vh), (ph, Vl), (pl, Vh))):
                            i = nc.tensor.matmul(dst, pr[p % 4][:, hp, :, :].rearrange("p w n -> p (w n)"),
                                                 v[upar][:, :, p, hp, :], start=(k == 0), stop=(k == 2))
                    i.then_inc(s_pv, 1)

                for s in range(PAIRS):
                    u, p = t_pair(t, s)
                    if exists(u):
                        t_scores(u, 1 - par if s >= TLAG else par, p)
                    if s + 1 < PAIRS and exists(t):
                        scores(t, par, s + 1)
                    if s + 1 == PAIRS and exists(t + 1):
                        scores(t + 1, 1 - par, 0)
                    if exists(t - 1) and s == 0:
                        pe.wait_ge(s_m16, done(t - 1))
                        pe.wait_ge(s_xT, done(t + 1))
                        nc.tensor.transpose(psT[:, 0:AP_], m16[:, :], idt[0:AP_, 0:AP_]).then_inc(s_mtp, 1)
                    if exists(t - 3) and s == 1:
                        pe.wait_ge(s_olo, done(t - 3))
                        pe.wait_ge(s_mT, done(t - 1))
                        for k in range(PAIRS):
                            i = nc.tensor.transpose(psT[:, k * FULL:k * FULL + AP_], otok[:, k, :], idt[0:AP_, 0:AP_])
                        i.then_inc(s_otp, 1)
                    u, p = v_pair(t, s)
                    if exists(u):
                        pv(u, 1 - par if s >= PLAG else par, p)
                    if exists(t + 1) and s < 4:
                        qk_piece(s)
                    if exists(t - 3) and s == 4:
                        pe.wait_ge(s_OT, done(t - 3))
                        lin_free(4)
                        for c in range(CH):
                            tok = OT[:, c * PT:c * PT + FULL]
                            dst = lin[:, c * C:(c + 1) * C]
                            nc.tensor.matmul(dst, tok, wh[:, WP:WP + C], start=True, stop=False)
                            i = nc.tensor.matmul(dst, tok, wl[:, WP:WP + C], start=False, stop=True)
                        i.then_inc(s_lin, 1)
                    if exists(t) and s == 5:
                        v_piece()
                    if exists(t + 2) and s == 7:
                        wait(pe, s_mT, done(t - 1))
                        wait(pe, s_OT, done(t - 3))
                        x_transposes(pe, t + 3)

            def prepare():
                pe.wait_ge(s_prep, 1)
            attention_phase(pe, step, prepare)

        @block.vector
        def _(dve):
            chain = [0]

            def link(i):
                chain[0] += 1
                i.then_inc(s_link, 1)
                dve.wait_ge(s_link, chain[0])

            for k in (*QAg, *KAg):
                nc.vector.memset(k[:, :, :, :], 0.0)
            for k in xT:
                nc.vector.memset(k[:, :, :], 0.0)
            nc.vector.memset(xtok[:, :, 2 * C:HL], SX)
            nc.vector.memset(xtok[:, :, HL:FULL], 0.0)
            nc.vector.memset(otok[:, :, 2 * C:HL], SO)
            nc.vector.memset(otok[:, :, HL:FULL], 0.0)
            nc.vector.memset(on[:, :, :], 0.0)
            nc.vector.memset(OT[:, TOK:TOK + FULL - PT], 0.0)
            for k in (*ph, *pl):
                nc.vector.memset(k[:, :, :, N:GP], 1.0)
            nc.vector.memset(m16[:, :], 0.0)
            flat = "p w n -> p (w n)"

            def step(t, par, late):
                new = 1 - par

                def k_low(j):
                    dve.wait_ge(s_high, 4 * done(t) + j + 1)
                    part = KA[new][GP:FULL, 8 * j:8 * j + 8, :].rearrange(flat)
                    nc.vector.scalar_tensor_tensor(part, lin[GP:FULL, 0:HALF], SQ / (SX * SWT), part,
                                                   ALU.mult, ALU.subtract).then_inc(s_linfree, 1)

                def q_low(j):
                    dve.wait_ge(s_high, 4 * done(t) + j + 3)
                    if j == 0:
                        wait(dve, s_qbh, done(t - 1))
                    nc.vector.scalar_tensor_tensor(QB[new][:, 8 * j:8 * j + 8, :].rearrange(flat), lin[:, 0:HALF],
                                                   SQ / (SX * SWT), QA[new][:, 8 * j:8 * j + 8, :].rearrange(flat),
                                                   ALU.mult, ALU.subtract).then_inc(s_linfree, 1)

                def v_low():
                    dve.wait_ge(s_vhigh, done(t))
                    for w in range(2):
                        for g in range(G):
                            i = nc.vector.scalar_tensor_tensor(v_dst(Vl, par, w, g), v_src(w, g), SV / (SX * SWT),
                                                               v_dst(Vh, par, w, g), ALU.mult, ALU.subtract)
                    i.then_inc(s_linfree, 1)

                def blocks(dst, src, rows, k):
                    return nc.vector.tensor_scalar(dst, src[:, :, :], rows[:, k:k + 1], None, ALU.mult)

                def rmax(p):
                    dve.wait_ge(s_s, PAIRS * t + p + 1)
                    if p == 0:
                        wait(dve, s_m16, done(t - 1))
                    nc.vector.tensor_reduce(rowmax[:, 2 * p:2 * p + 2, :],
                                            sc[p % 2][0:AP_, 0:2 * COLS].rearrange("p (a n) -> p a n", n=N),
                                            AX.X, ALU.max).then_inc(s_max, 1)

                def invert_sums(b):
                    dve.wait_ge(s_pv, PAIRS * (t - 2) + 4 * b + 4)
                    sums = po[b][0:AP_, 0:4 * HP * 2 * G * CP].rearrange("p (a d) -> p a d", d=CP)[:, :, HD]
                    nc.vector.reciprocal(rsum[:, b, :], sums).then_inc(s_rsum, 1)

                def normalize(b):
                    dve.wait_ge(s_rsum, 2 * (t - 2) + b + 1)
                    for w in range(2):
                        r = slice(w * GP, w * GP + N)
                        o = po[b][r, 0:4 * HP * 2 * G * CP].rearrange("p (a w g d) -> p a w g d", w=2, g=G, d=CP)[:, :, w, :, :]
                        dst = on[r, 4 * b:4 * b + 4, :].rearrange("p a (h g d) -> p (a h) g d", g=G, d=HD)
                        rs = rsum[r, b, :].rearrange("p (a w g) -> p a w g", w=2, g=G)[:, :, w, :]
                        i = nc.vector.tensor_tensor(dst, o[:, :, :, 0:HD], rs.unsqueeze(3).to_broadcast([N, 4 * HP, G, HD]),
                                                    ALU.mult)
                    i.then_inc(s_norm, 1)

                for s in range(PAIRS):
                    if exists(t + 2) and s == 0:
                        dve.wait_ge(s_x[par], 8 * (t + 2 - par) + 16)
                        ln_sum(dve, t + 2)
                    if exists(t + 2) and s == 3:
                        ln_sum_squares(dve, t + 3)
                    if exists(t - 2) and s in (2, 6):
                        invert_sums(s // 4)
                    if exists(t):
                        rmax(s)
                    if exists(t + 2) and s == 0:
                        ln_mean(dve, t + 3)
                    if exists(t + 2) and s == 3:
                        ln_variance(dve, t + 3)
                    if exists(t + 1):
                        if s == 1 or s == 2:
                            k_low(s - 1)
                        if s == 3 or s == 4:
                            q_low(s - 3)
                        if s == 3:
                            dve.wait_ge(s_linfree, lin_at(t, 1) + 1)
                            for hp in (0, 1):
                                blocks(KAh[new][:, hp, :, :], KA[new], headrow, hp)
                        if s == 4:
                            blocks(KAh[new][:, 2, :, :], KA[new], headrow, 2)
                            dve.wait_ge(s_high, 4 * done(t + 1))
                            for g in range(G):
                                i = blocks(QAg[new][:, :, g, 0:N], QA[new], grow, g)
                            i.then_inc(s_sb, 1)
                    if exists(t - 1) and s == 0:
                        dve.wait_ge(s_mtp, done(t - 1))
                        wait(dve, s_mrow, 16 * G * done(t - 2))
                        nc.vector.tensor_copy(mT[:, :], psT[0:HP * UW, 0:AP_]).then_inc(s_mT, 1)
                    if exists(t - 2) and s == 2:
                        normalize(0)
                    if exists(t - 3) and s == 5:
                        dve.wait_ge(s_lin, lin_at(t, 4) + 1)
                        y = lin[0:PT, 0:CH * C].rearrange("p (c n) -> p c n", n=C)
                        nc.vector.scalar_tensor_tensor(x_of(t - 3), y, 1.0 / (SO * SWT), x_of(t - 3),
                                                       ALU.mult, ALU.add).then_inc(s_linfree, 1)
                    if exists(t) and s == 5:
                        wait(dve, s_st, PAIRS * done(t - 2))
                        for g in range(G):
                            i = blocks(KAg[par][:, :, g, 0:N], KA[par], grow, g)
                        i.then_inc(s_tb, 1)
                    if exists(t - 2) and s == 6:
                        normalize(1)
                    if exists(t) and s == 6:
                        blocks(QAh[par][:, 0, :, :], QA[par], headrow, 0).then_inc(s_tb, 1)
                    if exists(t + 2) and s == 7:
                        ln_low(dve, t + 3)
                    if exists(t) and s == 7:
                        v_low()
                    if exists(t) and s == 7:
                        dve.wait_ge(s_max, PAIRS * done(t))
                        nc.vector.tensor_scalar(m16[:, 0:HP * UW].rearrange("p (a w) -> p a w", a=HP),
                                                rowmax[:, :, :].rearrange("p w a -> p a w"), -1.0 / SM, LOGP * SB / SM,
                                                ALU.mult, ALU.add).then_inc(s_m16, 1)
                    if exists(t - 2) and s == 7:
                        dve.wait_ge(s_ohi, done(t - 2))
                        nc.vector.tensor_tensor(otok[:, :, C:2 * C], on[:, :, :], otok[:, :, 0:C],
                                                ALU.subtract).then_inc(s_olo, 1)

            def prepare():
                dve.wait_ge(s_const, NCONST)
                dve.wait_ge(s_prep_p, 2)
                row = w32[2 * C:HL, :]
                link(nc.vector.tensor_tensor(row[:, 0:WF1], row[:, 0:WF1], banks[0][2 * C:HL, 0:WF1], ALU.add))
                link(nc.vector.tensor_tensor(row[:, WF1:WP], row[:, WF1:WP], banks[1][2 * C:HL, 0:WP - WF1], ALU.add))
                link(nc.vector.tensor_scalar(w32[0:2 * C, 0:WF1], w32[0:2 * C, 0:WF1], gain[:, 0:1], None, ALU.mult))
                link(nc.vector.tensor_scalar(w32[0:2 * C, WF1:WP], w32[0:2 * C, WF1:WP], gain[:, 1:2], None, ALU.mult))
                link(nc.vector.tensor_scalar(w32[:, WQ:WQ + FULL], w32[:, WQ:WQ + FULL], float(HD ** -0.5), None, ALU.mult))
                link(nc.vector.tensor_scalar(wh[:, :], w32[:, :], SWT, None, ALU.mult))
                link(nc.vector.scalar_tensor_tensor(wl[:, :], w32[:, :], SWT, wh[:, :], ALU.mult, ALU.subtract))
                link(nc.vector.tensor_scalar(w2h[:, :, :], w2f[:, :, :], SWT, None, ALU.mult))
                f = "p a n -> p (a n)"
                link(nc.vector.scalar_tensor_tensor(w2l[:, :, :].rearrange(f), w2f[:, :, :].rearrange(f), SWT,
                                                    w2h[:, :, :].rearrange(f), ALU.mult, ALU.subtract))
                for k, (hi, lo) in enumerate(((bs_h, None), (bt_h, bt_l))):
                    for a in range(4):
                        both = p32[a][:, 0, :, :].rearrange(f)
                        link(nc.vector.tensor_tensor(both, mask32[:, a, :], rpb32[:, k, :], ALU.add))
                        link(nc.vector.tensor_scalar(hi[:, a, :], both, SB, None, ALU.mult))
                        if lo is not None:
                            link(nc.vector.scalar_tensor_tensor(lo[:, a, :], both, SB, hi[:, a, :], ALU.mult, ALU.subtract))
                nc.vector.memset(rowmax[:, :, :], 0.0).then_inc(s_prep, 1)
            attention_phase(dve, step, prepare)

        actx.close()

        hT = [sb(f"hT{i}", [HL, TOK], f16) for i in range(2)]
        gel = sb("gel", [128, 3, HTOK], f32)
        gh = [sb(f"gh{i}", [128, 3, GW], f16) for i in range(2)]
        gl = [sb(f"gl{i}", [128, 3, GW], f16) for i in range(2)]
        ybuf = [sb(f"ybuf{i}", [PT, CH * C], f32) for i in range(2)]

        def mlp_phase(e, step):
            for t in range(-5, 3):
                step(t, t % 2)
            with e.Fori(3, UNITS - 8, 2) as i:
                step(i, 1)
                step(i + 1, 0)
            for t in range(UNITS - 7, UNITS + 1):
                step(t, t % 2)

        block = ctx.enter_context(nc.Block())

        @block.sync
        def _(sp):
            def step(t, par):
                if exists(t - 1):
                    sp.wait_ge(s_yo, done(t - 1))
                    sp.dma_start(out[bass.ds(t - 1, 1), :, :].rearrange("u p n -> p (u n)"),
                                 ybuf[1 - par][:, :]).then_inc(s_store[1 - par], 16)
            mlp_phase(sp, step)
            for par in range(2):
                sp.wait_ge(s_store[par], 16 * UNITS // 2)

        @block.gpsimd
        def _(pool):
            def step(t, par):
                n = t + 5 + UNITS
                if exists(t + 4):
                    ln_centre(pool, t + 4, par, n)
                if exists(t + 3):
                    ln_rsqrt(pool, n - 1)
                    ln_scale(pool, 1 - par, n - 1)
                if exists(t + 4):
                    nc.gpsimd.tensor_tensor(x_of(t + 4), x_of(t + 4), b2t[:, :].unsqueeze(1).to_broadcast([PT, CH, C]),
                                            ALU.add).then_inc(s_x1b, 1)
            mlp_phase(pool, step)

        @block.scalar
        def _(act):
            def step(t, par):
                def gelu(k):
                    act.wait_ge(s_h, 3 * t + k + 1)
                    wait(act, s_gl, 3 * (t - 1) + k + 1)
                    hb = banks[3 * par + k]
                    cols = HTOK if k == 0 else 3 * PT
                    if k == 0:
                        wait(act, s_y, t - 1)
                    for dst in (gh[par], gel):
                        i = nc.scalar.activation(dst[:, k, 0:cols], hb[:, 0:cols], ACT.Gelu, scale=1.0 / (SX * SWT))
                        if k == 2:
                            i = nc.scalar.activation(dst[0:64, k, cols:HTOK], hb[0:64, cols:HTOK], ACT.Gelu,
                                                     scale=1.0 / (SX * SWT))
                    i.then_inc(s_g, 1)

                n = t + 5 + UNITS
                if isinstance(t, int) and t == 0:
                    act.wait_ge(s_pads, 1)
                if exists(t + 2):
                    ln_high(act, n - 2)
                if exists(t):
                    gelu(0)
                if exists(t + 1):
                    act.wait_ge(s_xtp, n - 3)
                    nc.scalar.activation(hT[1 - par][:, :], psT[0:HL, 0:TOK], ACT.Copy).then_inc(s_xT, 1)
                if exists(t):
                    gelu(1)
                if exists(t + 4):
                    ln_square(act, par, n)
                if exists(t):
                    gelu(2)
            mlp_phase(act, step)

        @block.tensor
        def _(pe):
            def step(t, par):
                if exists(t):
                    pe.wait_ge(s_xT, t + 1 + UNITS)
                    wait(pe, s_g, 3 * (t - 1))
                    for k in range(2):
                        lo, hi = (0, HTOK) if k == 0 else (HTOK, TOK)
                        dst = banks[3 * par + k][:, 0:hi - lo]
                        nc.tensor.matmul(dst, wh[:, WF1:WF1 + FULL], hT[par][:, lo:hi], start=True, stop=False)
                        nc.tensor.matmul(dst, wl[:, WF1:WF1 + FULL], hT[par][:, lo:hi], start=False, stop=True).then_inc(s_h, 1)
                    for k in range(2):
                        lo, hi = (0, HTOK) if k == 0 else (HTOK, TOK)
                        col = WF1B + k * FULL
                        for m, wt in enumerate((wh, wl)):
                            i = nc.tensor.matmul(banks[3 * par + 2][:, 0:hi - lo], wt[:, col:col + FULL], hT[par][:, lo:hi],
                                                 start=(k == 0 and m == 0), stop=(k == 1 and m == 1), skip_group_check=True)
                    i.then_inc(s_h, 1)
                if exists(t - 1):
                    pe.wait_ge(s_gl, 3 * t)
                    wait(pe, s_yo, t - 1)
                    for c in range(CH):
                        k, at = c // 4, (c % 4) * PT
                        dst = banks[6][:, c * C:(c + 1) * C]
                        terms = [(a[1 - par], r, wt, j) for r, j in ((k, 0), (2, 1 + k))
                                 for a, wt in ((gh, w2h), (gh, w2l), (gl, w2h))]
                        for m, (a, r, wt, j) in enumerate(terms):
                            i = nc.tensor.matmul(dst, a[:, r, at:at + FULL], wt[:, j, :], start=(m == 0), stop=(m == 5))
                    i.then_inc(s_y, 1)
                if exists(t + 2):
                    pe.wait_ge(s_xT, t + 2 + UNITS)
                    x_transposes(pe, t + 3 + UNITS)
            mlp_phase(pe, step)

        @block.vector
        def _(dve):
            nc.vector.memset(gel[64:128, 2, 3 * PT:HTOK], 0.0)
            for k in (*gh, *gl):
                i = nc.vector.memset(k[:, :, :], 0.0)
            i.then_inc(s_pads, 1)

            def step(t, par):
                def split(k):
                    dve.wait_ge(s_g, 3 * t + k + 1)
                    cols = 3 * PT if k == 1 else HTOK
                    nc.vector.tensor_tensor(gl[par][:, k, 0:cols], gel[:, k, 0:cols], gh[par][:, k, 0:cols],
                                            ALU.subtract).then_inc(s_gl, 1)

                n = t + 5 + UNITS
                if exists(t):
                    split(0)
                if exists(t + 2):
                    ln_low(dve, n - 2)
                if exists(t):
                    split(1)
                if exists(t + 5):
                    dve.wait_ge(s_xc, n)
                    ln_sum(dve, t + 5)
                    ln_mean(dve, n + 1)
                if exists(t):
                    split(2)
                if exists(t + 4):
                    ln_sum_squares(dve, n)
                    dve.wait_ge(s_pow, n)
                    ln_variance(dve, n)
                if exists(t - 1):
                    dve.wait_ge(s_y, done(t - 1))
                    dve.wait_ge(s_x1b, done(t - 1))
                    wait(dve, s_store[1 - par], 8 * (t - 1 - (1 - par)))
                    nc.vector.scalar_tensor_tensor(ybuf[1 - par][:, :].rearrange("p (c n) -> p c n", n=C),
                                                   banks[6][0:PT, 0:CH * C].rearrange("p (c n) -> p c n", n=C),
                                                   1.0 / SWT, x_of(t - 1), ALU.mult, ALU.add).then_inc(s_yo, 1)
            mlp_phase(dve, step)


def _windows(x):
    x = np.roll(x, (-SS, -SS), axis=(1, 2)).reshape(B, H // WS, WS, NWX, WS, C)
    x = x.transpose(1, 0, 3, 2, 4, 5).reshape(UNITS, CH, PT, C)
    return np.ascontiguousarray(x.transpose(0, 2, 1, 3)).reshape(UNITS, PT, CH * C)


def _image(y):
    y = y.reshape(UNITS, PT, CH, C).transpose(0, 2, 1, 3).reshape(H // WS, B, NWX, WS, WS, C)
    y = y.transpose(1, 0, 3, 2, 4, 5).reshape(B, H, W, C)
    return np.ascontiguousarray(np.roll(y, (SS, SS), axis=(1, 2)))


def _weights(qkv_w, qkv_b, proj_w, proj_b, fc1_w, fc1_b):
    def stack(w, b):
        return np.concatenate([w, w, b[None]], axis=0)

    qkv = stack(qkv_w, qkv_b)
    w = np.zeros((HL, WCOLS), np.float32)
    for k, at in enumerate((WQ, WK)):
        cols = qkv[:, k * C:(k + 1) * C].reshape(HL, HP, G, HD)
        for quadrant in range(4):
            c = at + quadrant * KQ
            w[:, c:c + KD] = cols[:, :, quadrant % 2, :].reshape(HL, KD)
    w[2 * C, WK + MROW:WK + MROW + G] = SM / SQ
    w[:, WV:WV + C] = qkv[:, 2 * C:3 * C]
    fc1 = stack(fc1_w, fc1_b)
    w[:, WF1:WF1 + 128] = fc1[:, 0:128]
    w[:, WF1B:WF1B + 64] = fc1[:, 128:HID]
    w[:, WF1B + FULL + 64:WF1B + 2 * FULL] = fc1[:, 128:HID]
    w[:, WP:WP + C] = stack(proj_w, proj_b)
    return w


def _position_bias(table):
    i = np.arange(N)
    r, c = i // WS, i % WS
    at = (r[:, None] - r[None, :] + WS - 1) * (2 * WS - 1) + (c[:, None] - c[None, :] + WS - 1)
    out = np.zeros((AP_, 2, HP, N), np.float32)
    for g in range(G):
        for hp in range(HP):
            m = table[:, 2 * hp + g][at]
            out[g * GP:g * GP + N, 0, hp] = m
            out[g * GP:g * GP + N, 1, hp] = m.T
    return out.reshape(AP_, 2, COLS)


def _window_mask():
    out = np.zeros((AP_, 4, HP, N), np.float32)
    i = np.arange(N)
    for kind in range(4):
        row = (i // WS >= WS - SS) if kind // 2 else np.zeros(N, bool)
        col = (i % WS >= WS - SS) if kind % 2 else np.zeros(N, bool)
        region = 2 * row + col
        m = np.where(region[:, None] != region[None, :], -100.0, 0.0)
        for g in range(G):
            out[g * GP:g * GP + N, kind] = m[:, None, :]
    return out.reshape(AP_, 4, COLS)


def kernel(**inputs):
    import concourse.bacc as bacc
    from concourse.bass_utils import run_bass_kernel_spmd

    p = {k.replace("L0_conv_", ""): np.asarray(v) for k, v in inputs.items()}
    shifts = np.zeros((C, 2, HL), np.float32)
    shifts[:, 0, 2 * C] = p["norm1_b"]
    shifts[:, 1, 2 * C] = p["norm2_b"]
    gains = np.stack([np.concatenate([p[k]] * 2) for k in ("norm1_g", "norm2_g")], axis=1)
    headrow = np.zeros((FULL, HP), np.float32)
    grow = np.zeros((FULL, G), np.float32)
    for quadrant in range(4):
        for hp in range(HP):
            headrow[quadrant * KQ + hp * HD:quadrant * KQ + (hp + 1) * HD, hp] = 1.0
        grow[quadrant * KQ:quadrant * KQ + KD, quadrant % 2] = 1.0
    for g in range(G):
        grow[MROW + g, g] = 1.0
    w2 = np.zeros((128, 3, C), np.float32)
    w2[:, 0] = p["fc2_w"][0:128]
    for k in range(2):
        w2[64 * k:64 * k + 64, 1 + k] = p["fc2_w"][128:HID]
    onescol = np.zeros((2, AP_, 2, PAIRS, HP, G, CP), np.float16)
    for g in range(G):
        onescol[0, g * GP:g * GP + N, :, :, :, g, HD] = SV / SO
    arrays = {
        "x": _windows(p["x"]),
        "weights": _weights(p["qkv_w"], p["qkv_b"], p["proj_w"], p["proj_b"], p["fc1_w"], p["fc1_b"]),
        "gains": gains,
        "shifts": shifts,
        "w2": w2,
        "b2": np.ascontiguousarray(np.broadcast_to(p["fc2_b"], (PT, C))),
        "rpb": _position_bias(p["rpb_table"]),
        "headrow": headrow,
        "grow": grow,
        "maskt": _window_mask(),
        "ident": np.eye(128, dtype=np.float16),
        "onescol": onescol.reshape(2, AP_, 2, PAIRS, HP, G * CP),
    }
    nc = bacc.Bacc("TRN2", target_bir_lowering=False, num_devices=1)
    args = [nc.dram_tensor(f"in_{k}", a.shape, mybir.dt.from_np(a.dtype), kind="ExternalInput").ap()
            for k, a in arrays.items()]
    out = nc.dram_tensor("out_y", (UNITS, PT, CH * C), mybir.dt.float32, kind="ExternalOutput").ap()
    swin_block_kernel(nc, *args, out)
    r = run_bass_kernel_spmd(nc, [{f"in_{k}": a for k, a in arrays.items()}], core_ids=[0])
    return _image(r.results[0]["out_y"])
```
